# Optimizing a Trainium2 kernel written in Bass

```python
import numpy as np
import jax
import jax.numpy as jnp

def _softmax(x, axis=-1):
    return jax.nn.softmax(x, axis=axis)

def _gelu(x):
    return jax.nn.gelu(x, approximate=True)

def _silu(x):
    return jax.nn.silu(x)

def _sigmoid(x):
    return jax.nn.sigmoid(x)

def _layernorm(x, axis=-1, eps=1e-05):
    m = jnp.mean(x, axis=axis, keepdims=True)
    v = jnp.var(x, axis=axis, keepdims=True)
    return (x - m) / jnp.sqrt(v + eps)

def _scatter_add(tgt, idx, src, axis=0):
    return tgt.at[idx].add(src)

def _segment_sum(src, seg, n):
    return jax.ops.segment_sum(src, seg, n)
kernel_name = 'mk_adj_resnorm_d4_adj_r2_9e907a'

def setup_inputs(seed: int=0):
    np.random.seed(seed)
    _w = jnp.asarray

    def _rec_inputs():
        import jax
        import jax.numpy as jnp
        _gk = jax.random.key(seed)
        x = -0.0003929 + 0.9999 * jax.random.normal(jax.random.fold_in(_gk, 1), (128, 128, 256), jnp.float32)
        _a = jax.random.bernoulli(jax.random.fold_in(_gk, 2), 0.125, (128, 128, 128))
        _a = jnp.logical_or(_a, jnp.swapaxes(_a, -1, -2))
        _a = jnp.logical_or(_a, jnp.eye(128, dtype=bool))
        _af = _a.astype(jnp.float32)
        _af = _af * jax.random.uniform(jax.random.fold_in(_gk, 3), (128, 128, 128), jnp.float32, 0.05, 1)
        adj = _af
        _nm = jnp.ones((128, 128), dtype=bool)
        nodemask = _nm
        return (x, adj, nodemask)
    x, adj, nodemask = _rec_inputs()

    def _L0_gnn_setup():
        import jax, jax.numpy as jnp
        import numpy as np
        EPS = 1e-06
        key = jax.random.key(seed)
        k1, k2, k3 = jax.random.split(key, 3)
        B, N, F, O = (8, 2048, 256, 256)
        x = jax.random.normal(k1, (B, N, F), dtype=jnp.float32)
        adj = jax.random.uniform(k2, (B, N, N), dtype=jnp.float32)
        W = jax.random.normal(k3, (O, 2 * F), dtype=jnp.float32) * (1.0 / np.sqrt(2 * F))
        return {'x': x, 'adj': adj, 'W': W}
    _L0_gnn_all = _L0_gnn_setup()
    _L0_gnn_in = {k: v for k, v in _L0_gnn_all.items() if k in ('W',)}
    del _L0_gnn_all

    def _L1_gnn_setup():
        import jax, jax.numpy as jnp
        import numpy as np
        B, N, DIN, DOUT = (8, 1024, 256, 256)
        EDGE_P = 0.01

        def _gcn_norm(adj):
            A = (adj != 0).astype(adj.dtype)
            eye = jnp.eye(A.shape[-1], dtype=A.dtype)
            A = jnp.maximum(A, eye)
            deg = A.sum(axis=-1)
            dinv = jnp.where(deg > 0, jax.lax.rsqrt(deg), 0.0)
            return dinv[..., :, None] * A * dinv[..., None, :]
        key = jax.random.key(seed)
        k1, k2, k3, k4 = jax.random.split(key, 4)
        inputs = jax.random.normal(k1, (B, N, DIN), dtype=jnp.float32)
        adj = (jax.random.uniform(k2, (B, N, N)) < EDGE_P).astype(jnp.float32)
        W = jax.random.normal(k3, (DIN, DOUT), dtype=jnp.float32) / np.sqrt(DIN)
        b = jax.random.normal(k4, (DOUT,), dtype=jnp.float32) * 0.01
        return {'inputs': inputs, 'adj': adj, 'W': W, 'b': b}
    _L1_gnn_all = _L1_gnn_setup()
    _L1_gnn_in = {k: v for k, v in _L1_gnn_all.items() if k in ('W', 'b')}
    del _L1_gnn_all

    def _L2_gnn_setup():
        import jax, jax.numpy as jnp
        import numpy as np
        HEADS = 8
        DIM_HEAD = 64
        LA = 0.33
        LD = 0.33
        LG = 0.33
        key = jax.random.key(seed)
        ks = jax.random.split(key, 6)
        B, N, D = (4, 512, 256)
        inner = HEADS * DIM_HEAD
        x = jax.random.normal(ks[0], (B, N, D), jnp.float32)
        mask = jax.random.uniform(ks[1], (B, N)) < 0.9
        adjacency_mat = (jax.random.uniform(ks[2], (B, N, N)) < 0.05).astype(jnp.float32)
        distance_mat = jax.random.uniform(ks[3], (B, N, N), jnp.float32) * 5.0
        W_qkv = jax.random.normal(ks[4], (D, inner * 3), jnp.float32) * 0.02
        W_out = jax.random.normal(ks[5], (inner, D), jnp.float32) * 0.02
        b_out = jnp.zeros((D,), jnp.float32)
        return {'x': x, 'mask': mask, 'adjacency_mat': adjacency_mat, 'distance_mat': distance_mat, 'W_qkv': W_qkv, 'W_out': W_out, 'b_out': b_out}
    _L2_gnn_all = _L2_gnn_setup()
    _L2_gnn_in = {k: v for k, v in _L2_gnn_all.items() if k in ('W_qkv', 'W_out', 'b_out')}
    del _L2_gnn_all

    def _L3_gnn_setup():
        import jax, jax.numpy as jnp
        import numpy as np
        B, N, DIN, DOUT, K = (4, 1024, 256, 256, 3)
        key = jax.random.key(seed)
        ks = jax.random.split(key, 8)
        X = jax.random.normal(ks[0], (B, N, DIN), dtype=jnp.float32)
        A = jax.random.uniform(ks[1], (B, N, N), dtype=jnp.float32)
        Wv = jax.random.normal(ks[2], (DIN, DOUT), dtype=jnp.float32) * 0.02
        bv = jax.random.normal(ks[3], (DOUT,), dtype=jnp.float32) * 0.02
        aw = jax.random.normal(ks[4], (2 * DOUT, 1), dtype=jnp.float32) * 0.05
        ab = jax.random.normal(ks[5], (1,), dtype=jnp.float32) * 0.05
        Wk = jax.random.normal(ks[6], (K, DIN, DOUT), dtype=jnp.float32) * 0.02
        bk = jax.random.normal(ks[7], (K, DOUT), dtype=jnp.float32) * 0.02
        return {'X': X, 'A': A, 'Wv': Wv, 'bv': bv, 'aw': aw, 'ab': ab, 'Wk': Wk, 'bk': bk}
    _L3_gnn_all = _L3_gnn_setup()
    _L3_gnn_in = {k: v for k, v in _L3_gnn_all.items() if k in ('Wv', 'bv', 'aw', 'ab', 'Wk', 'bk')}
    del _L3_gnn_all
    return {'x': x, 'adj': adj, 'nodemask': nodemask, 'L0_gnn_W': _L0_gnn_in['W'], 'L1_gnn_W': _L1_gnn_in['W'], 'L1_gnn_b': _L1_gnn_in['b'], 'L2_gnn_W_qkv': _L2_gnn_in['W_qkv'], 'L2_gnn_W_out': _L2_gnn_in['W_out'], 'L2_gnn_b_out': _L2_gnn_in['b_out'], 'L3_gnn_Wv': _L3_gnn_in['Wv'], 'L3_gnn_bv': _L3_gnn_in['bv'], 'L3_gnn_aw': _L3_gnn_in['aw'], 'L3_gnn_ab': _L3_gnn_in['ab'], 'L3_gnn_Wk': _L3_gnn_in['Wk'], 'L3_gnn_bk': _L3_gnn_in['bk']}

def reference(x, adj, nodemask, L0_gnn_W, L1_gnn_W, L1_gnn_b, L2_gnn_W_qkv, L2_gnn_W_out, L2_gnn_b_out, L3_gnn_Wv, L3_gnn_bv, L3_gnn_aw, L3_gnn_ab, L3_gnn_Wk, L3_gnn_bk):
    import jax
    import jax.numpy as jnp

    def _L0_gnn_ref(x, adj, W):
        import jax, jax.numpy as jnp
        import numpy as np
        EPS = 1e-06
        deg = jnp.sum(adj, axis=-1, keepdims=True)
        agg = jnp.einsum('bij,bjf->bif', adj, x) / jnp.maximum(deg, EPS)
        cat = jnp.concatenate([x, agg], axis=2)
        out = jnp.einsum('bnf,of->bno', cat, W)
        return jax.nn.relu(out)

    def _L1_gnn_ref(inputs, adj, W, b):
        import jax, jax.numpy as jnp
        import numpy as np
        B, N, DIN, DOUT = (8, 1024, 256, 256)
        EDGE_P = 0.01

        def _gcn_norm(adj):
            A = (adj != 0).astype(adj.dtype)
            eye = jnp.eye(A.shape[-1], dtype=A.dtype)
            A = jnp.maximum(A, eye)
            deg = A.sum(axis=-1)
            dinv = jnp.where(deg > 0, jax.lax.rsqrt(deg), 0.0)
            return dinv[..., :, None] * A * dinv[..., None, :]
        norm = _gcn_norm(adj)
        h = jnp.einsum('bnf,fo->bno', inputs, W)
        agg = jnp.einsum('bnm,bmo->bno', norm, h)
        return jnp.tanh(agg + b)

    def _L2_gnn_ref(x, mask, adjacency_mat, distance_mat, W_qkv, W_out, b_out):
        import jax, jax.numpy as jnp
        import numpy as np
        HEADS = 8
        DIM_HEAD = 64
        LA = 0.33
        LD = 0.33
        LG = 0.33
        B, N, _ = x.shape
        scale = DIM_HEAD ** (-0.5)
        qkv = (x @ W_qkv).reshape(B, N, HEADS, 3, DIM_HEAD)
        q, k, v = (jnp.transpose(qkv[..., i, :], (0, 2, 1, 3)) for i in range(3))
        dots = jnp.einsum('bhid,bhjd->bhij', q, k) * scale
        big = jnp.finfo(dots.dtype).max
        m2 = mask[:, None, :, None] & mask[:, None, None, :]
        dots = jnp.where(m2, dots, -big)
        attn = jax.nn.softmax(dots, axis=-1) * LA
        adj = jnp.where(m2, adjacency_mat[:, None], 0.0)
        dist = jnp.where(m2, distance_mat[:, None], big)
        attn = attn + LG * adj + LD * jnp.exp(-dist)
        out = jnp.einsum('bhij,bhjd->bhid', attn, v)
        out = jnp.transpose(out, (0, 2, 1, 3)).reshape(B, N, HEADS * DIM_HEAD)
        return out @ W_out + b_out

    def _L3_gnn_ref(X, A, Wv, bv, aw, ab, Wk, bk):
        import jax, jax.numpy as jnp
        import numpy as np
        B, N, DIN, DOUT, K = (4, 1024, 256, 256, 3)
        d = Wv.shape[1]
        Xw = X @ Wv + bv
        sj = Xw @ aw[:d, 0]
        si = Xw @ aw[d:, 0]
        e = jax.nn.leaky_relu(sj[:, None, :] + si[:, :, None] + ab[0], negative_slope=0.2)
        alpha_matrix = A * jnp.exp(e)
        transition = alpha_matrix / (jnp.sum(alpha_matrix, axis=-1, keepdims=True) + 1e-12)
        H = jnp.zeros(X.shape[:-1] + (d,), dtype=X.dtype)
        Xk = X
        for k in range(Wk.shape[0]):
            H = H + Xk @ Wk[k] + bk[k]
            Xk = jnp.einsum('bij,bjd->bid', transition, Xk)
        return jax.nn.relu(H)
    x = _layernorm(x + _L0_gnn_ref(x, adj, L0_gnn_W), axis=-1)
    x = _layernorm(x + _L1_gnn_ref(x, adj, L1_gnn_W, L1_gnn_b), axis=-1)
    x = _layernorm(x + _L2_gnn_ref(x, nodemask, adj, adj, L2_gnn_W_qkv, L2_gnn_W_out, L2_gnn_b_out), axis=-1)
    x = _layernorm(x + _L3_gnn_ref(x, adj, L3_gnn_Wv, L3_gnn_bv, L3_gnn_aw, L3_gnn_ab, L3_gnn_Wk, L3_gnn_bk), axis=-1)
    return x

_drawn_inputs = setup_inputs


def setup_inputs(seed=0):
    import zlib

    import numpy as np

    out = dict(_drawn_inputs(seed))
    spreads = {'L2_gnn_b_out': (0.0, 0.1)}
    factors = {}
    for name, (base, spread) in spreads.items():
        noise = np.random.default_rng([zlib.crc32(name.encode()), seed]).standard_normal(out[name].shape)
        drawn = base * np.exp(spread * noise) if base else spread * noise
        out[name] = jnp.asarray(drawn.astype(out[name].dtype))
    for name, factor in factors.items():
        out[name] = (out[name] * factor).astype(out[name].dtype)
    return out
```

```python
import concourse.bass as bass
from concourse import mybir
from contextlib import ExitStack

F32 = mybir.dt.float32
F16 = mybir.dt.float16
BF16 = mybir.dt.bfloat16
U8 = mybir.dt.uint8
ALU = mybir.AluOpType
ACT = mybir.ActivationFunctionType
AX = mybir.AxisListType.X

P = 128
G = 2
F = 256
FT = F // P
HEADS = 8
DH = 64
HP = HEADS // 2
INNER = HEADS * DH
HOPS = 3
WS = 256.0
LAMBDA = 0.33
SCALE = DH ** -0.5
BIG = 1e30
LN_EPS = 1e-5
DEG_EPS = 1e-6
SUM_EPS = 1e-12

SEMS = """
ident_made weights_loaded consts_loaded setup_hi setup_lo setup_psum setup_moved setup_dve setup_pool
x0_loaded adj0_loaded mask_loaded adj3_loaded out_stored
deg_summed deg_clamped deg_inverted adjn_made edges_counted dinv_made
x0t_done a0t_done xt0_hi xt0_lo adjnt_made at_made
ag_done agt_hi agt_lo l0_done relu0_made y0_made
x1_made y1_made ya_done yt_hi yt_lo h1_done z_made tanh_made y1b_made x2_made sdinv_made
mask_rows mask_tiles exp_adj_made c0_made c_rows c_made xt2_done xt2_hi xt2_lo xb_made
qk_done q_made k_made v_done v_made d_done negmax_made exps_made rsum_made pn_made attn_made
tr_done pt_made pv_done ot_hi ot_lo wo_done y2_made x3_made
xt3_done xt3_hi xt3_lo e3_done w2_done si_made e_made leaky_made expe_made m_made ssum_made rs_made tn_made
mt_done tt_made hw2_made t1_done u1_made t0_done relu3_made y3_made xo_made
bn0 bn1 bn2 bn3 aggr0 aggr1 aggr2 aggr3 vare0 vare1 vare2 vare3 rstd0 rstd1 rstd2 rstd3
""".split()


def build(nc, x, adj, nodemask, w0, w1, b1, wqkv, wout, bout, wv, bv, aw, ab, wk, bk, out):
    GRAPHS = x.shape[0]
    PAIRS = GRAPHS // G
    assert x.shape[1:] == (P, F) and GRAPHS % G == 0 and GRAPHS == P and PAIRS >= 4

    x_pair = x.rearrange("(t g) n f -> t n g f", g=G)
    adj_pair = adj.rearrange("(t g) n m -> t n g m", g=G)
    out_pair = out.rearrange("(t g) n f -> t n g f", g=G)
    mask_pair = nodemask.rearrange("(t g) n -> t (g n)", g=G)

    with ExitStack() as ctx:
        def sb(name, shape, dt=F32):
            return ctx.enter_context(nc.sbuf_tensor(name, shape, dt))

        s = {n: ctx.enter_context(nc.semaphore(n)) for n in SEMS}

        ident = sb("ident", [P, P])
        raw0 = sb("raw0", [P, FT, 2 * F])
        raw1 = sb("raw1", [P, FT, F])
        rawq = sb("rawq", [P, FT, 3 * INNER])
        rawo = sb("rawo", [P, HP, F])
        rawk = sb("rawk", [P, FT, HOPS, F])
        rawv = sb("rawv", [P, FT, F])
        wvt = sb("wvt", [P, FT, F])
        acol = sb("acol", [P, 2 * FT])
        asum = sb("asum", [P, FT])
        bvcol = sb("bvcol", [P, FT])
        bvrep = sb("bvrep", [P, FT, P])
        arep = sb("arep", [P, FT, P])
        abc = sb("abc", [P, 1])
        econst = sb("econst", [P, 1])
        b1bc = sb("b1bc", [P, F])
        bobc = sb("bobc", [P, F])
        bkrow = sb("bkrow", [1, HOPS, F])
        bksum = sb("bksum", [1, F])
        bksum2 = sb("bksum2", [1, F])
        epsln = sb("epsln", [P, G])
        mhalf = sb("mhalf", [P, G])
        mask8all = sb("mask8all", [P, P], U8)
        maskf = sb("maskf", [P, P])
        maskt = sb("maskt", [P, P])
        ones16 = sb("ones16", [1, P], F16)

        def pair_of_parts(name, shape):
            return sb(name + "_hi", shape, F16), sb(name + "_lo", shape, F16)

        w0t = pair_of_parts("w0t", [P, 2 * FT, F])
        w1p = pair_of_parts("w1p", [P, FT, F])
        wq = pair_of_parts("wq", [P, FT, HP, P])
        wkk = pair_of_parts("wkk", [P, FT, HP, P])
        wvv = pair_of_parts("wvv", [P, FT, INNER])
        wo = pair_of_parts("wo", [P, HP, F])
        wl = pair_of_parts("wl", [P, FT, HOPS, F])
        wj = pair_of_parts("wj", [P, FT, P])
        wi = pair_of_parts("wi", [P, FT, 1])
        bks = pair_of_parts("bks", [1, F])

        x0 = sb("x0", [P, G, F])
        adj0 = sb("adj0", [P, G, P])
        deg = sb("deg", [P, G])
        degc = sb("degc", [P, G])
        rdeg = sb("rdeg", [P, G])
        adjn = sb("adjn", [P, G, P])
        edges = sb("edges", [P, G, P])
        nedges = sb("nedges", [P, G])
        dinv = sb("dinv", [P, G])
        sdinv = sb("sdinv", [P, G])
        xt0 = pair_of_parts("xt0", [P, FT, G, P])
        adjnt = sb("adjnt", [P, G, P])
        at = sb("at", [P, G, P])
        agt = pair_of_parts("agt", [P, FT, G, P])
        relu0 = sb("relu0", [P, G, F])
        y0 = sb("y0", [P, G, F])
        x1 = sb("x1", [P, G, F])
        y1 = sb("y1", [P, G, F])
        yt = pair_of_parts("yt", [P, FT, G, P])
        z1 = sb("z1", [P, G, F])
        tanh1 = sb("tanh1", [P, G, F])
        y1b = sb("y1b", [P, G, F])
        x2 = sb("x2", [P, G, F])
        mask8 = sb("mask8", [P, G, P], U8)
        maskbc = sb("maskbc", [P, G, P])
        maskcol = sb("maskcol", [P, G])
        maskrow = sb("maskrow", [1, G, P], BF16)
        bigrow = sb("bigrow", [1, G, P], BF16)
        expadj = sb("expadj", [P, G, P])
        c0 = sb("c0", [P, G, P])
        crow = sb("crow", [P, G, P])
        c2 = sb("c2", [P, G, P])
        xt2 = pair_of_parts("xt2", [P, FT, G, P])
        xb = sb("xb", [P, G, F])
        qt = sb("qt", [P, 2, G, P])
        kt = sb("kt", [P, 2, G, 2, P])
        vv = sb("vv", [P, G, INNER])
        negmax = sb("negmax", [P, 2, G * 2])
        rowsum = sb("rowsum", [P, 2, G * 2])
        rrow = sb("rrow", [P, 2, G * 2])
        probs = sb("probs", [P, 2, G * 2, P])
        pn = sb("pn", [P, 2, G * 2, P])
        attn = sb("attn", [P, 2, G, 2, P])
        pt = sb("pt", [P, G, 2, P])
        ot = pair_of_parts("ot", [P, HP, G, P])
        y2 = sb("y2", [P, G, F])
        x3 = sb("x3", [P, G, F])
        adj3 = sb("adj3", [P, G, P])
        xt3 = pair_of_parts("xt3", [P, FT, G, P])
        si = sb("si", [P, G])
        ee = sb("ee", [P, G, P])
        leaky = sb("leaky", [P, G, P])
        expe = sb("expe", [P, G, P])
        mm = sb("mm", [P, G, P])
        ssum = sb("ssum", [P, G])
        ssume = sb("ssume", [P, G])
        rs = sb("rs", [P, G])
        tn = sb("tn", [P, G, P])
        tt = sb("tt", [P, G, P])
        hw2 = sb("hw2", [P, G, F])
        u1 = sb("u1", [P, G, F])
        relu3 = sb("relu3", [P, G, F])
        y3 = sb("y3", [P, G, F])
        xo = sb("xo", [P, G, F])
        stats = sb("stats", [P, 4, G, 6])
        mv = sb("mv", [P, 4, G, 2])
        vare = sb("vare", [P, 4, G])
        rstd = sb("rstd", [P, 4, G])

        def bank(name):
            return ctx.enter_context(nc.psum_tensor(name, [P, 512], F32))

        QK, VB, DA, DB, TP, O1, O2, O3 = (bank(n) for n in ("QK", "VB", "DA", "DB", "TP", "O1", "O2", "O3"))
        SC = (DA, DB)

        def v4(b):
            return b[:, :].rearrange("p (a g n) -> p a g n", a=2, g=G)

        def v3(b):
            return b[:, :].rearrange("p (g f) -> p g f", g=G)

        def half(b, k):
            return b[:, k * 256:(k + 1) * 256].rearrange("p (g n) -> p g n", g=G)

        def hold(eng, sem, n):
            if not (isinstance(n, int) and n <= 0):
                eng.wait_ge(sem, n)

        def stand_alone(eng):
            eng.wait_ge(s["ident_made"], 1)

        qkv_head = rawq[:, :, :].rearrange("p t (h s d) -> p t h s d", s=3, d=DH)

        def schedule(eng, step):
            step(0, True, None)
            with eng.Fori(1, PAIRS - 1) as t:
                step(t, True, True)
            step(PAIRS - 1, None, True)

        block = ctx.enter_context(nc.Block())

        @block.sync
        def _(sp):
            for dst, src in ((raw0[:, :, :], w0.rearrange("(t p) f -> p t f", p=P)),
                             (raw1[:, :, :], w1.rearrange("(t p) f -> p t f", p=P)),
                             (rawq[:, :, :], wqkv.rearrange("(t p) f -> p t f", p=P)),
                             (rawo[:, :, :], wout.rearrange("(t p) f -> p t f", p=P)),
                             (rawv[:, :, :], wv.rearrange("(t p) f -> p t f", p=P))):
                sp.dma_start(dst, src).then_inc(s["weights_loaded"], 16)
            for k in range(HOPS):
                sp.dma_start(rawk[:, :, k, :], wk[k].rearrange("(t p) f -> p t f", p=P)).then_inc(s["weights_loaded"], 16)

            def load_layer0(p):
                stand_alone(sp)
                hold(sp, s["ag_done"], p)
                hold(sp, s["y0_made"], p)
                sp.dma_start(x0[:, :, :], x_pair[p]).then_inc(s["x0_loaded"], 16)
                stand_alone(sp)
                hold(sp, s["a0t_done"], p)
                hold(sp, s["edges_counted"], p)
                hold(sp, s["c0_made"], p)
                sp.dma_start(adj0[:, :, :], adj_pair[p]).then_inc(s["adj0_loaded"], 16)

            def load_adj3(p):
                stand_alone(sp)
                hold(sp, s["m_made"], p)
                sp.dma_start(adj3[:, :, :], adj_pair[p]).then_inc(s["adj3_loaded"], 16)

            def store(p):
                stand_alone(sp)
                sp.wait_ge(s["xo_made"], p + 1)
                sp.dma_start(out_pair[p], xo[:, :, :]).then_inc(s["out_stored"], 16)

            load_layer0(0)
            load_adj3(0)
            load_layer0(1)
            load_layer0(2)
            with sp.Fori(1, PAIRS - 2) as t:
                load_layer0(t + 2)
                load_adj3(t)
                store(t - 1)
            load_adj3(PAIRS - 2)
            store(PAIRS - 3)
            load_adj3(PAIRS - 1)
            store(PAIRS - 2)
            store(PAIRS - 1)
            sp.wait_ge(s["out_stored"], 16 * PAIRS)

        @block.gpsimd
        def _(pool):
            pool.memset(ident[:, :], 0.0).then_inc(s["setup_pool"], 1)
            pool.wait_ge(s["setup_pool"], 1)
            pool.affine_select(out=ident[:, :], in_=ident[:, :], compare_op=ALU.not_equal, fill=1.0,
                               base=0, pattern=[[-1, P]], channel_multiplier=1).then_inc(s["ident_made"], 1)
            pool.memset(epsln[:, :], LN_EPS).then_inc(s["setup_pool"], 1)
            pool.memset(mhalf[:, :], -0.5).then_inc(s["setup_pool"], 1)
            pool.memset(ones16[:, :], 1.0).then_inc(s["setup_pool"], 1)
            pool.memset(kt[:, :, :, :, :], 0.0).then_inc(s["setup_pool"], 1)
            pool.wait_ge(s["setup_pool"], 5)
            pool.wait_ge(s["setup_moved"], 3)

            def bias_and_masks(p):
                pool.wait_ge(s["mask_loaded"], 16 * (p + 1))
                hold(pool, s["d_done"], 4 * p)
                hold(pool, s["q_made"], 4 * p)
                hold(pool, s["c_made"], p)
                pool.wait_ge(s["x2_made"], p + 1)
                hold(pool, s["y2_made"], p)
                pool.tensor_tensor(xb[:, :, :], x2[:, :, :], bobc[:, :].unsqueeze(1).to_broadcast([P, G, F]),
                                   ALU.add).then_inc(s["xb_made"], 1)
                pool.tensor_copy(maskrow[:, :, :], mask8[0:1, :, :]).then_inc(s["mask_rows"], 1)
                pool.tensor_scalar(bigrow[:, :, :], mask8[0:1, :, :], -BIG, BIG, ALU.mult, ALU.add).then_inc(s["mask_rows"], 1)
                pool.tensor_copy(maskcol[:, :], maskt[:, bass.ds(p * G, G)]).then_inc(s["mask_rows"], 1)
                pool.tensor_copy(maskbc[:, :, :], mask8[:, :, :]).then_inc(s["mask_tiles"], 1)

            def distance(p):
                pool.wait_ge(s["exp_adj_made"], p + 1)
                hold(pool, s["c_rows"], p)
                pool.tensor_tensor(c0[:, :, :], adj0[:, :, :], expadj[:, :, :], ALU.add).then_inc(s["c0_made"], 1)

            def inv_sqrt_degree(p):
                pool.wait_ge(s["edges_counted"], p + 1)
                hold(pool, s["z_made"], p)
                pool.tensor_tensor(dinv[:, :], nedges[:, :], mhalf[:, :], ALU.pow).then_inc(s["dinv_made"], 1)

            def residual(p, made, out_t, a, b, a_made, out_read):
                pool.wait_ge(a_made, p + 1)
                hold(pool, out_read, p)
                pool.tensor_tensor(out_t[:, :, :], a[:, :, :], b[:, :, :], ALU.add).then_inc(made, 1)

            def rstd_of(layer, p, aggr, vare_s, rstd_s):
                pool.wait_ge(aggr, p + 1)
                pool.tensor_tensor(vare[:, layer, :], mv[:, layer, :, 1], epsln[:, :], ALU.add).then_inc(vare_s, 1)
                pool.wait_ge(vare_s, p + 1)
                pool.tensor_tensor(rstd[:, layer, :], vare[:, layer, :], mhalf[:, :], ALU.pow).then_inc(rstd_s, 1)

            def residual0(p):
                pool.wait_ge(s["x0_loaded"], 16 * (p + 1))
                residual(p, s["y0_made"], y0, relu0, x0, s["relu0_made"], s["x1_made"])

            def add_c(p, h):
                pool.wait_ge(s["pn_made"], 4 * p + h + 1)
                if h == 0:
                    pool.wait_ge(s["c_made"], p + 1)
                hold(pool, s["tr_done"], 4 * p + h - 1)
                pool.tensor_tensor(attn[:, h % 2], pn[:, h % 2].rearrange("p (g e) n -> p g e n", g=G),
                                   c2[:, :, :].unsqueeze(2).to_broadcast([P, G, 2, P]), ALU.add).then_inc(s["attn_made"], 1)

            def layer01_start(p):
                inv_sqrt_degree(p)
                distance(p)

            def step(t, has01, has3):
                a, b, c = t + 1, t, t - 1
                bias_and_masks(b)
                if has01:
                    layer01_start(a)
                add_c(b, 0)
                if has01:
                    residual0(a)
                    rstd_of(0, a, s["aggr0"], s["vare0"], s["rstd0"])
                add_c(b, 1)
                add_c(b, 2)
                if has01:
                    residual(a, s["y1b_made"], y1b, tanh1, x1, s["tanh_made"], s["x2_made"])
                    rstd_of(1, a, s["aggr1"], s["vare1"], s["rstd1"])
                add_c(b, 3)
                if has3:
                    residual(c, s["y3_made"], y3, relu3, x3, s["relu3_made"], s["xo_made"])
                    rstd_of(3, c, s["aggr3"], s["vare3"], s["rstd3"])
                rstd_of(2, b, s["aggr2"], s["vare2"], s["rstd2"])

            layer01_start(0)
            residual0(0)
            rstd_of(0, 0, s["aggr0"], s["vare0"], s["rstd0"])
            residual(0, s["y1b_made"], y1b, tanh1, x1, s["tanh_made"], s["x2_made"])
            rstd_of(1, 0, s["aggr1"], s["vare1"], s["rstd1"])
            schedule(pool, step)
            residual(PAIRS - 1, s["y3_made"], y3, relu3, x3, s["relu3_made"], s["xo_made"])
            rstd_of(3, PAIRS - 1, s["aggr3"], s["vare3"], s["rstd3"])

        @block.scalar
        def _(act):
            act.dma_start(acol[:, :], aw.rearrange("(t p) o -> p (t o)", p=P), allow_slow_non_contiguous=True).then_inc(s["consts_loaded"], 16)
            act.dma_start(bvcol[:, :], bv.rearrange("(t p) -> p t", p=P), allow_slow_non_contiguous=True).then_inc(s["consts_loaded"], 16)
            act.dma_start(abc[:, :], ab.partition_broadcast(P)).then_inc(s["consts_loaded"], 16)
            act.dma_start(b1bc[:, :], b1.partition_broadcast(P)).then_inc(s["consts_loaded"], 16)
            act.dma_start(bobc[:, :], bout.partition_broadcast(P)).then_inc(s["consts_loaded"], 16)
            act.dma_start(bkrow[:, :, :], bk.unsqueeze(0)).then_inc(s["consts_loaded"], 16)
            act.dma_start(mask8all[:, :], nodemask).then_inc(s["consts_loaded"], 16)

            act.wait_ge(s["weights_loaded"], 16 * 8)
            act.activation(w1p[0][:, :, :], raw1[:, :, :], ACT.Copy, scale=WS).then_inc(s["setup_hi"], 1)
            act.activation(wo[0][:, :, :], rawo[:, :, :], ACT.Copy, scale=WS).then_inc(s["setup_hi"], 1)
            act.activation(wl[0][:, :, :, :], rawk[:, :, :, :], ACT.Copy, scale=WS).then_inc(s["setup_hi"], 1)
            for k in range(FT):
                for part, w in ((0, wq), (1, wkk)):
                    act.activation(w[0][:, k, :, :].rearrange("p h (e d) -> p (h e) d", e=2),
                                   qkv_head[:, k, :, part, :], ACT.Copy, scale=WS).then_inc(s["setup_hi"], 1)
                act.activation(wvv[0][:, k, :].rearrange("p (h d) -> p h d", h=HEADS),
                               qkv_head[:, k, :, 2, :], ACT.Copy, scale=WS).then_inc(s["setup_hi"], 1)
            act.wait_ge(s["setup_psum"], 1)
            act.activation(w0t[0][:, 0:2, :], v3(DA), ACT.Copy, scale=WS).then_inc(s["setup_hi"], 1)
            act.activation(w0t[0][:, 2:4, :], v3(DB), ACT.Copy, scale=WS).then_inc(s["setup_hi"], 1)
            act.wait_ge(s["setup_psum"], 4)
            act.activation(wj[0][:, :, :], half(O2, 0), ACT.Copy, scale=WS).then_inc(s["setup_hi"], 1)
            act.activation(wi[0][:, :, 0], O2[:, 256:258], ACT.Copy, scale=WS).then_inc(s["setup_hi"], 1)
            act.wait_ge(s["setup_dve"], 4)
            act.activation(bks[0][:, :], bksum2[:, :], ACT.Copy, scale=WS).then_inc(s["setup_hi"], 1)

            def high(p, hi, src, done, made):
                act.wait_ge(done, p + 1)
                act.activation(hi[:, :, :, :], v4(src), ACT.Copy).then_inc(made, 1)

            def adjn_t(p):
                act.wait_ge(s["a0t_done"], p + 1)
                act.activation(adjnt[:, :, :], half(O2, 0), ACT.Copy).then_inc(s["adjnt_made"], 1)

            def exp_adj(p):
                act.wait_ge(s["adj0_loaded"], 16 * (p + 1))
                hold(act, s["c0_made"], p)
                act.activation(expadj[:, :, :], adj0[:, :, :], ACT.Exp, scale=-1.0).then_inc(s["exp_adj_made"], 1)

            def relu_of(p, dst, src, done, made, read):
                act.wait_ge(done, p + 1)
                hold(act, read, p)
                act.activation(dst[:, :, :], v3(src), ACT.Relu, scale=1.0 / WS).then_inc(made, 1)

            def relu_0(p):
                relu_of(p, relu0, O3, s["l0_done"], s["relu0_made"], s["y0_made"])

            def relu_3(p):
                relu_of(p, relu3, O3, s["t0_done"], s["relu3_made"], s["y3_made"])

            def tanh_1(p):
                act.wait_ge(s["z_made"], p + 1)
                hold(act, s["y1b_made"], p)
                act.activation(tanh1[:, :, :], z1[:, :, :], ACT.Tanh).then_inc(s["tanh_made"], 1)

            def key(p, h):
                act.wait_ge(s["q_made"], 4 * p + h + 1)
                for e in range(2):
                    rows = slice(e * DH, (e + 1) * DH)
                    last = act.activation(kt[rows, h % 2, :, e, :], QK[rows, 256:512].rearrange("p (g n) -> p g n", g=G),
                                          ACT.Copy, scale=1.0 / WS)
                last.then_inc(s["k_made"], 1)

            def value(p, g):
                act.wait_ge(s["v_done"], 2 * p + g + 1)
                act.activation(vv[:, g, :], VB[:, :], ACT.Copy, scale=LAMBDA / WS).then_inc(s["v_made"], 1)

            def exps(p, h):
                act.wait_ge(s["negmax_made"], 4 * p + h + 1)
                hold(act, s["pn_made"], 4 * p + h - 1)
                for ge in range(2 * G):
                    last = act.activation(probs[:, h % 2, ge, :], SC[h % 2][:, ge * P:(ge + 1) * P], ACT.Exp,
                                          scale=-1.0, bias=negmax[:, h % 2, ge:ge + 1],
                                          accum_out=rowsum[:, h % 2, ge:ge + 1])
                last.then_inc(s["exps_made"], 1)

            def attn_t(p, h):
                act.wait_ge(s["tr_done"], 4 * p + h + 1)
                act.activation(pt[:, :, :, :], v4(TP), ACT.Copy).then_inc(s["pt_made"], 1)

            def out_high(p, h):
                act.wait_ge(s["pv_done"], 4 * p + h + 1)
                act.activation(ot[0][:, h], half(TP, 0), ACT.Copy).then_inc(s["ot_hi"], 1)

            def hop2(p):
                act.wait_ge(s["w2_done"], p + 1)
                act.activation(hw2[:, :, :], v3(O1), ACT.Copy).then_inc(s["hw2_made"], 1)

            def exp_e(p):
                act.wait_ge(s["leaky_made"], p + 1)
                hold(act, s["m_made"], p)
                act.activation(expe[:, :, :], leaky[:, :, :], ACT.Exp).then_inc(s["expe_made"], 1)

            def transition_t(p):
                act.wait_ge(s["mt_done"], p + 1)
                act.activation(tt[:, :, :], half(O1, 0), ACT.Copy).then_inc(s["tt_made"], 1)

            def hop1(p):
                act.wait_ge(s["t1_done"], p + 1)
                act.activation(u1[:, :, :], v3(O2), ACT.Copy).then_inc(s["u1_made"], 1)

            def load_mask(p):
                hold(act, s["mask_tiles"], p)
                act.dma_start(mask8[:, :, :].rearrange("p g n -> p (g n)"),
                              mask_pair[p].partition_broadcast(P)).then_inc(s["mask_loaded"], 16)

            def layer01_a(p):
                high(p, xt0[0], O1, s["x0t_done"], s["xt0_hi"])
                adjn_t(p)
                exp_adj(p)

            def layer01_b(p):
                high(p, agt[0], O1, s["ag_done"], s["agt_hi"])

            def step(t, has01, has3):
                a, b, c = t + 1, t, t - 1
                high(b, xt2[0], TP, s["xt2_done"], s["xt2_hi"])
                if has01:
                    layer01_a(a)
                key(b, 0)
                value(b, 0)
                if has01:
                    layer01_b(a)
                exps(b, 0)
                key(b, 1)
                value(b, 1)
                if has01:
                    load_mask(a)
                exps(b, 1)
                if has01:
                    relu_0(a)
                if has3:
                    high(c, xt3[0], O1, s["xt3_done"], s["xt3_hi"])
                attn_t(b, 0)
                key(b, 2)
                out_high(b, 0)
                exps(b, 2)
                if has3:
                    exp_e(c)
                    hop2(c)
                attn_t(b, 1)
                if has01:
                    high(a, yt[0], VB, s["ya_done"], s["yt_hi"])
                key(b, 3)
                out_high(b, 1)
                exps(b, 3)
                if has01:
                    tanh_1(a)
                if has3:
                    transition_t(c)
                attn_t(b, 2)
                if has3:
                    hop1(c)
                out_high(b, 2)
                attn_t(b, 3)
                if has3:
                    relu_3(c)
                out_high(b, 3)

            act.wait_ge(s["setup_pool"], 5)
            load_mask(0)
            layer01_a(0)
            layer01_b(0)
            relu_0(0)
            high(0, yt[0], VB, s["ya_done"], s["yt_hi"])
            tanh_1(0)
            schedule(act, step)
            q = PAIRS - 1
            high(q, xt3[0], O1, s["xt3_done"], s["xt3_hi"])
            exp_e(q)
            hop2(q)
            transition_t(q)
            hop1(q)
            relu_3(q)

        @block.vector
        def _(dve):
            def low(w_lo, src, w_hi):
                return dve.scalar_tensor_tensor(out=w_lo, in0=src, scalar=WS, in1=w_hi,
                                                op0=ALU.mult, op1=ALU.subtract).then_inc(s["setup_lo"], 1)

            dve.wait_ge(s["consts_loaded"], 16 * 7)
            dve.tensor_copy(maskf[:, :], mask8all[:, :]).then_inc(s["setup_dve"], 1)
            dve.tensor_copy(bvrep[:, :, :], bvcol[:, :].unsqueeze(2).to_broadcast([P, FT, P])).then_inc(s["setup_moved"], 1)
            dve.tensor_copy(arep[:, :, :], acol[:, 0:FT].unsqueeze(2).to_broadcast([P, FT, P])).then_inc(s["setup_dve"], 1)
            dve.tensor_tensor(bksum[:, :], bkrow[:, 0, :], bkrow[:, 1, :], ALU.add).then_inc(s["setup_dve"], 1)
            dve.wait_ge(s["setup_dve"], 3)
            dve.tensor_tensor(bksum2[:, :], bksum[:, :], bkrow[:, 2, :], ALU.add).then_inc(s["setup_dve"], 1)
            dve.tensor_tensor(asum[:, :], acol[:, 0:FT], acol[:, FT:2 * FT], ALU.add).then_inc(s["setup_dve"], 1)
            dve.wait_ge(s["setup_psum"], 2)
            dve.tensor_copy(wvt[:, :, :], v3(O1)).then_inc(s["setup_moved"], 1)
            dve.wait_ge(s["setup_psum"], 3)
            dve.tensor_copy(maskt[:, :], O3[:, 0:P]).then_inc(s["setup_moved"], 1)
            dve.wait_ge(s["setup_hi"], 9)
            low(w1p[1][:, :, :], raw1[:, :, :], w1p[0][:, :, :])
            low(wo[1][:, :, :], rawo[:, :, :], wo[0][:, :, :])
            low(wl[1][:, :, :, :].rearrange("p t k f -> p (t k f)"), rawk[:, :, :, :].rearrange("p t k f -> p (t k f)"),
                wl[0][:, :, :, :].rearrange("p t k f -> p (t k f)"))
            for k in range(FT):
                for part, w in ((0, wq), (1, wkk)):
                    low(w[1][:, k, :, :].rearrange("p h (e d) -> p (h e) d", e=2), qkv_head[:, k, :, part, :],
                        w[0][:, k, :, :].rearrange("p h (e d) -> p (h e) d", e=2))
                low(wvv[1][:, k, :].rearrange("p (h d) -> p h d", h=HEADS), qkv_head[:, k, :, 2, :],
                    wvv[0][:, k, :].rearrange("p (h d) -> p h d", h=HEADS))
            dve.wait_ge(s["setup_hi"], 11)
            low(w0t[1][:, 0:2, :], v3(DA), w0t[0][:, 0:2, :])
            low(w0t[1][:, 2:4, :], v3(DB), w0t[0][:, 2:4, :])
            dve.wait_ge(s["setup_hi"], 14)
            low(wj[1][:, :, :], half(O2, 0), wj[0][:, :, :])
            low(wi[1][:, :, 0], O2[:, 256:258], wi[0][:, :, 0])
            dve.tensor_scalar(econst[:, :], O2[:, 258:259], abc[:, :], None, ALU.add).then_inc(s["setup_lo"], 1)
            low(bks[1][:, :], bksum2[:, :], bks[0][:, :])

            def rest(p, lo, hi, src, hi_made, made):
                dve.wait_ge(hi_made, p + 1)
                dve.tensor_tensor(lo[:, :, :, :], v4(src), hi[:, :, :, :], ALU.subtract).then_inc(made, 1)

            def normalised_adjacency(p):
                dve.wait_ge(s["adj0_loaded"], 16 * (p + 1))
                dve.tensor_reduce(deg[:, :], adj0[:, :, :], AX, ALU.add).then_inc(s["deg_summed"], 1)
                hold(dve, s["dinv_made"], p)
                for g in range(G):
                    last = dve.scalar_tensor_tensor(out=edges[:, g, :], in0=adj0[:, g, :], scalar=0.0, in1=ident[:, :],
                                                    op0=ALU.not_equal, op1=ALU.max, accum_out=nedges[:, g:g + 1])
                last.then_inc(s["edges_counted"], 1)
                dve.wait_ge(s["deg_summed"], p + 1)
                dve.tensor_scalar(degc[:, :], deg[:, :], DEG_EPS, None, ALU.max).then_inc(s["deg_clamped"], 1)
                dve.wait_ge(s["deg_clamped"], p + 1)
                dve.reciprocal(rdeg[:, :], degc[:, :]).then_inc(s["deg_inverted"], 1)
                dve.wait_ge(s["deg_inverted"], p + 1)
                hold(dve, s["a0t_done"], p)
                for g in range(G):
                    last = dve.tensor_scalar(adjn[:, g, :], adj0[:, g, :], rdeg[:, g:g + 1], None, ALU.mult)
                last.then_inc(s["adjn_made"], 1)

            def edges_t(p):
                dve.wait_ge(s["adjnt_made"], p + 1)
                dve.scalar_tensor_tensor(out=at[:, :, :], in0=half(O2, 1), scalar=0.0,
                                         in1=ident[:, :].unsqueeze(1).to_broadcast([P, G, P]),
                                         op0=ALU.not_equal, op1=ALU.max).then_inc(s["at_made"], 1)

            def norm_stats(layer, p, src, made, bn, aggr):
                dve.wait_ge(made, p + 1)
                for g in range(G):
                    last = dve.bn_stats(stats[:, layer, g, :], src[:, g, :])
                last.then_inc(bn, 1)
                stand_alone(dve)
                dve.wait_ge(bn, p + 1)
                for g in range(G):
                    last = dve.bn_aggr(mv[:, layer, g, :], stats[:, layer, g, :])
                last.then_inc(aggr, 1)

            def norm_apply(layer, p, dst, src, rstd_s, made):
                dve.wait_ge(rstd_s, p + 1)
                for g in range(G):
                    last = dve.tensor_scalar(dst[:, g, :], src[:, g, :], mv[:, layer, g, 0:1], rstd[:, layer, g:g + 1],
                                             ALU.subtract, ALU.mult)
                last.then_inc(made, 1)

            def ln0_stats(p):
                norm_stats(0, p, y0, s["y0_made"], s["bn0"], s["aggr0"])

            def ln0_apply(p):
                hold(dve, s["y1b_made"], p)
                norm_apply(0, p, x1, y0, s["rstd0"], s["x1_made"])
                dve.wait_ge(s["dinv_made"], p + 1)
                dve.wait_ge(s["x1_made"], p + 1)
                dve.tensor_scalar(sdinv[:, :], dinv[:, :], 1.0 / WS, None, ALU.mult).then_inc(s["sdinv_made"], 1)
                for g in range(G):
                    last = dve.tensor_scalar(y1[:, g, :], x1[:, g, :], dinv[:, g:g + 1], None, ALU.mult)
                last.then_inc(s["y1_made"], 1)

            def before_tanh(p):
                dve.wait_ge(s["h1_done"], p + 1)
                dve.wait_ge(s["sdinv_made"], p + 1)
                for g in range(G):
                    last = dve.scalar_tensor_tensor(out=z1[:, g, :], in0=VB[:, g * F:(g + 1) * F], scalar=sdinv[:, g:g + 1],
                                                    in1=b1bc[:, :], op0=ALU.mult, op1=ALU.add)
                last.then_inc(s["z_made"], 1)

            def ln1_stats(p):
                norm_stats(1, p, y1b, s["y1b_made"], s["bn1"], s["aggr1"])

            def ln1_apply(p):
                hold(dve, s["xb_made"], p)
                norm_apply(1, p, x2, y1b, s["rstd1"], s["x2_made"])

            def masked_c(p):
                dve.wait_ge(s["mask_tiles"], p + 1)
                dve.wait_ge(s["c0_made"], p + 1)
                for g in range(G):
                    last = dve.tensor_scalar(crow[:, g, :], c0[:, g, :], maskcol[:, g:g + 1], None, ALU.mult)
                last.then_inc(s["c_rows"], 1)
                dve.wait_ge(s["c_rows"], p + 1)
                hold(dve, s["attn_made"], 4 * p)
                dve.tensor_tensor(c2[:, :, :], crow[:, :, :], maskbc[:, :, :], ALU.mult).then_inc(s["c_made"], 1)

            def query(p, h):
                dve.wait_ge(s["qk_done"], 4 * p + h + 1)
                if h == 0:
                    dve.wait_ge(s["mask_tiles"], p + 1)
                dve.scalar_tensor_tensor(out=qt[:, h % 2], in0=half(QK, 0), scalar=-SCALE / WS, in1=maskbc[:, :, :],
                                         op0=ALU.mult, op1=ALU.mult).then_inc(s["q_made"], 1)

            def minus_max(p, h):
                dve.wait_ge(s["d_done"], 4 * p + h + 1)
                dve.tensor_reduce(negmax[:, h % 2, :], SC[h % 2][:, :].rearrange("p (a n) -> p a n", n=P), AX,
                                  ALU.min).then_inc(s["negmax_made"], 1)

            def normalise(p, h):
                dve.wait_ge(s["exps_made"], 4 * p + h + 1)
                dve.reciprocal(rrow[:, h % 2, :], rowsum[:, h % 2, :]).then_inc(s["rsum_made"], 1)
                dve.wait_ge(s["rsum_made"], 4 * p + h + 1)
                hold(dve, s["attn_made"], 4 * p + h - 1)
                dve.tensor_tensor(pn[:, h % 2], probs[:, h % 2],
                                  rrow[:, h % 2, :].unsqueeze(2).to_broadcast([P, 2 * G, P]), ALU.mult).then_inc(s["pn_made"], 1)

            def out_low(p, h):
                dve.wait_ge(s["ot_hi"], 4 * p + h + 1)
                dve.tensor_tensor(ot[1][:, h], half(TP, 0), ot[0][:, h], ALU.subtract).then_inc(s["ot_lo"], 1)

            def residual2(p):
                dve.wait_ge(s["wo_done"], p + 1)
                dve.wait_ge(s["xb_made"], p + 1)
                dve.scalar_tensor_tensor(out=y2[:, :, :], in0=v3(QK), scalar=1.0 / WS, in1=xb[:, :, :],
                                         op0=ALU.mult, op1=ALU.add).then_inc(s["y2_made"], 1)

            def ln2_stats(p):
                norm_stats(2, p, y2, s["y2_made"], s["bn2"], s["aggr2"])

            def ln2_apply(p):
                hold(dve, s["y3_made"], p)
                norm_apply(2, p, x3, y2, s["rstd2"], s["x3_made"])

            def exponent(p):
                dve.wait_ge(s["e3_done"], p + 1)
                dve.tensor_scalar(si[:, :], O2[:, 256:258], 1.0 / WS, econst[:, :], ALU.mult, ALU.add).then_inc(s["si_made"], 1)
                dve.wait_ge(s["si_made"], p + 1)
                for g in range(G):
                    last = dve.tensor_scalar(ee[:, g, :], O2[:, g * P:(g + 1) * P], 1.0 / WS, si[:, g:g + 1], ALU.mult, ALU.add)
                last.then_inc(s["e_made"], 1)
                dve.wait_ge(s["e_made"], p + 1)
                dve.scalar_tensor_tensor(out=leaky[:, :, :], in0=ee[:, :, :], scalar=0.2, in1=ee[:, :, :],
                                         op0=ALU.mult, op1=ALU.max).then_inc(s["leaky_made"], 1)

            def transition(p):
                dve.wait_ge(s["expe_made"], p + 1)
                dve.wait_ge(s["adj3_loaded"], 16 * (p + 1))
                for g in range(G):
                    last = dve.scalar_tensor_tensor(out=mm[:, g, :], in0=expe[:, g, :], scalar=1.0, in1=adj3[:, g, :],
                                                    op0=ALU.mult, op1=ALU.mult, accum_out=ssum[:, g:g + 1])
                last.then_inc(s["m_made"], 1)
                dve.wait_ge(s["m_made"], p + 1)
                dve.tensor_scalar(ssume[:, :], ssum[:, :], SUM_EPS, None, ALU.add).then_inc(s["ssum_made"], 1)
                dve.wait_ge(s["ssum_made"], p + 1)
                dve.reciprocal(rs[:, :], ssume[:, :]).then_inc(s["rs_made"], 1)
                dve.wait_ge(s["rs_made"], p + 1)
                hold(dve, s["mt_done"], p)
                for g in range(G):
                    last = dve.tensor_scalar(tn[:, g, :], mm[:, g, :], rs[:, g:g + 1], None, ALU.mult)
                last.then_inc(s["tn_made"], 1)

            def ln3_stats(p):
                norm_stats(3, p, y3, s["y3_made"], s["bn3"], s["aggr3"])

            def ln3_apply(p):
                hold(dve, s["out_stored"], 16 * p)
                norm_apply(3, p, xo, y3, s["rstd3"], s["xo_made"])

            def step(t, has01, has3, more=True):
                a, b, c = t + 1, t, t - 1
                rest(b, xt2[1], xt2[0], TP, s["xt2_hi"], s["xt2_lo"])
                if has01:
                    rest(a, xt0[1], xt0[0], O1, s["xt0_hi"], s["xt0_lo"])
                    edges_t(a)
                masked_c(b)
                query(b, 0)
                minus_max(b, 0)
                if has01:
                    rest(a, agt[1], agt[0], O1, s["agt_hi"], s["agt_lo"])
                query(b, 1)
                normalise(b, 0)
                minus_max(b, 1)
                if has3:
                    rest(c, xt3[1], xt3[0], O1, s["xt3_hi"], s["xt3_lo"])
                if has01:
                    ln0_stats(a)
                query(b, 2)
                normalise(b, 1)
                if has01:
                    ln0_apply(a)
                out_low(b, 0)
                minus_max(b, 2)
                if has3:
                    exponent(c)
                query(b, 3)
                if has01:
                    rest(a, yt[1], yt[0], VB, s["yt_hi"], s["yt_lo"])
                if has3:
                    transition(c)
                normalise(b, 2)
                out_low(b, 1)
                minus_max(b, 3)
                if has01:
                    before_tanh(a)
                out_low(b, 2)
                if has01:
                    ln1_stats(a)
                normalise(b, 3)
                if has01:
                    ln1_apply(a)
                if has01 and more:
                    normalised_adjacency(a + 1)
                if has3:
                    ln3_stats(c)
                out_low(b, 3)
                if has3:
                    ln3_apply(c)
                residual2(b)
                ln2_stats(b)
                ln2_apply(b)

            dve.wait_ge(s["ident_made"], 1)
            normalised_adjacency(0)
            rest(0, xt0[1], xt0[0], O1, s["xt0_hi"], s["xt0_lo"])
            edges_t(0)
            rest(0, agt[1], agt[0], O1, s["agt_hi"], s["agt_lo"])
            ln0_stats(0)
            ln0_apply(0)
            rest(0, yt[1], yt[0], VB, s["yt_hi"], s["yt_lo"])
            before_tanh(0)
            ln1_stats(0)
            ln1_apply(0)
            normalised_adjacency(1)
            step(0, True, None)
            with dve.Fori(1, PAIRS - 2) as t:
                step(t, True, True)
            step(PAIRS - 2, True, True, more=False)
            step(PAIRS - 1, None, True)
            q = PAIRS - 1
            rest(q, xt3[1], xt3[0], O1, s["xt3_hi"], s["xt3_lo"])
            exponent(q)
            transition(q)
            ln3_stats(q)
            ln3_apply(q)

        @block.tensor
        def _(pe):
            def product(dst, lhs, rhs, k, first=False, last=False):
                for n, (i, j) in enumerate(((0, 0), (0, 1), (1, 0))):
                    mm_ = pe.matmul(dst, lhs(i, k), rhs(j, k), start=first and n == 0, stop=last and n == 2,
                                    skip_group_check=True)
                return mm_

            pe.wait_ge(s["ident_made"], 1)
            pe.wait_ge(s["weights_loaded"], 16 * 8)
            for c in range(2 * FT):
                for o in range(FT):
                    dst = (DA, DB)[c // 2][:, (c % 2) * F + o * P:(c % 2) * F + (o + 1) * P]
                    last = pe.transpose(dst, raw0[:, o, c * P:(c + 1) * P], ident[:, :])
            last.then_inc(s["setup_psum"], 1)
            for d in range(FT):
                for f in range(FT):
                    last = pe.transpose(O1[:, d * F + f * P:d * F + (f + 1) * P], rawv[:, f, d * P:(d + 1) * P], ident[:, :])
            last.then_inc(s["setup_psum"], 1)
            pe.wait_ge(s["setup_dve"], 5)
            pe.transpose(O3[:, 0:P], maskf[:, :], ident[:, :]).then_inc(s["setup_psum"], 1)
            pe.wait_ge(s["setup_moved"], 2)
            for f in range(FT):
                for d in range(FT):
                    pe.matmul(O2[:, f * P:(f + 1) * P], wvt[:, d, f * P:(f + 1) * P], arep[:, d, :],
                              start=f == 0 and d == 0, stop=d == 1, skip_group_check=True)
                for d in range(FT):
                    pe.matmul(O2[:, 256 + f:257 + f], wvt[:, d, f * P:(f + 1) * P], acol[:, FT + d:FT + d + 1],
                              start=False, stop=d == 1, skip_group_check=True)
            for d in range(FT):
                last = pe.matmul(O2[:, 258:259], bvrep[:, d, :], asum[:, d:d + 1], start=False, stop=d == 1,
                                 skip_group_check=True)
            last.then_inc(s["setup_psum"], 1)
            pe.wait_ge(s["setup_lo"], 15)
            pe.wait_ge(s["setup_pool"], 5)

            def transposes(p, src, dst, ready, done, n=1):
                pe.wait_ge(ready, n * (p + 1))
                for k in range(FT):
                    for g in range(G):
                        last = pe.transpose(dst[:, (k * G + g) * P:(k * G + g + 1) * P], src[:, g, k * P:(k + 1) * P], ident[:, :])
                last.then_inc(done, 1)

            def adjacency_t(p):
                pe.wait_ge(s["adjn_made"], p + 1)
                for k, src in enumerate((adjn, adj0)):
                    for g in range(G):
                        last = pe.transpose(O2[:, (k * G + g) * P:(k * G + g + 1) * P], src[:, g, :], ident[:, :])
                last.then_inc(s["a0t_done"], 1)

            def nodes_by_weights(p, dst, lhs, rhs, ks, first, wgt0=0):
                for g in range(G):
                    for k in ks:
                        last = product(dst[:, g * F:(g + 1) * F], lambda i, k: lhs[i][:, k, g, :],
                                       lambda j, k: rhs[j][:, wgt0 + k, :], k,
                                       first=first and g == 0 and k == ks[0], last=k == ks[-1])
                return last

            def aggregate0(p):
                pe.wait_ge(s["adjnt_made"], p + 1)
                pe.wait_ge(s["xt0_lo"], p + 1)
                for k in range(FT):
                    for g in range(G):
                        last = pe.matmul(O1[:, (k * G + g) * P:(k * G + g + 1) * P], x0[:, g, k * P:(k + 1) * P], adjnt[:, g, :],
                                         start=k == 0 and g == 0, stop=True, skip_group_check=True)
                last.then_inc(s["ag_done"], 1)

            def layer0_x(p):
                hold(pe, s["relu3_made"], p - 2)
                nodes_by_weights(p, O3, xt0, w0t, range(FT), True)

            def layer0_agg(p):
                pe.wait_ge(s["agt_lo"], p + 1)
                pe.wait_ge(s["at_made"], p + 1)
                nodes_by_weights(p, O3, agt, w0t, range(FT), False, wgt0=FT).then_inc(s["l0_done"], 1)

            def aggregate1(p):
                pe.wait_ge(s["y1_made"], p + 1)
                for k in range(FT):
                    for g in range(G):
                        last = pe.matmul(VB[:, (k * G + g) * P:(k * G + g + 1) * P], y1[:, g, k * P:(k + 1) * P], at[:, g, :],
                                         start=k == 0 and g == 0, stop=True, skip_group_check=True)
                last.then_inc(s["ya_done"], 1)

            def layer1(p):
                pe.wait_ge(s["yt_lo"], p + 1)
                nodes_by_weights(p, VB, yt, w1p, range(FT), True).then_inc(s["h1_done"], 1)

            def project_qk(p, h):
                if h == 0:
                    pe.wait_ge(s["xt2_lo"], p + 1)
                    hold(pe, s["y2_made"], p)
                for part, w in enumerate((wq, wkk)):
                    for k in range(FT):
                        last = product(QK[:, part * 256:(part + 1) * 256], lambda i, k: w[i][:, k, h, :],
                                       lambda j, k: xt2[j][:, k].rearrange("p g n -> p (g n)"), k,
                                       first=part == 0 and k == 0, last=k == FT - 1)
                last.then_inc(s["qk_done"], 1)

            def project_v(p, g):
                if g == 1:
                    pe.wait_ge(s["v_made"], 2 * p + 1)
                for k in range(FT):
                    last = product(VB[:, :], lambda i, k: xt2[i][:, k, g, :], lambda j, k: wvv[j][:, k, :], k,
                                   first=k == 0, last=k == FT - 1)
                last.then_inc(s["v_done"], 1)

            def scores(p, h):
                if h == 0:
                    pe.wait_ge(s["mask_rows"], 3 * (p + 1))
                pe.wait_ge(s["k_made"], 4 * p + h + 1)
                bank_ = SC[h % 2]
                for g in range(G):
                    pe.matmul(bank_[:, g * 256:(g + 1) * 256], maskrow[0:1, g, :],
                              bigrow[0:1, g:g + 1, :].to_broadcast([1, 2, P]), start=g == 0, stop=False, skip_group_check=True)
                for g in range(G):
                    last = pe.matmul(bank_[:, g * 256:(g + 1) * 256], qt[:, h % 2, g, :],
                                     kt[:, h % 2, g].rearrange("p e n -> p (e n)"), start=False, stop=True,
                                     skip_group_check=True)
                last.then_inc(s["d_done"], 1)

            def attention_t(p, h):
                pe.wait_ge(s["attn_made"], 4 * p + h + 1)
                if h > 0:
                    pe.wait_ge(s["ot_lo"], 4 * p + h)
                for g in range(G):
                    for e in range(2):
                        last = pe.transpose(TP[:, (2 * g + e) * P:(2 * g + e + 1) * P], attn[:, h % 2, g, e, :], ident[:, :])
                last.then_inc(s["tr_done"], 1)

            def apply_attention(p, h):
                pe.wait_ge(s["pt_made"], 4 * p + h + 1)
                if h == 0:
                    pe.wait_ge(s["v_made"], 2 * p + 2)
                for g in range(G):
                    for e in range(2):
                        head = 2 * h + e
                        last = pe.matmul(TP[e * DH:(e + 1) * DH, g * P:(g + 1) * P], vv[:, g, head * DH:(head + 1) * DH],
                                         pt[:, g, e, :], start=True, stop=True, skip_group_check=True)
                last.then_inc(s["pv_done"], 1)

            def project_out(p):
                pe.wait_ge(s["ot_lo"], 4 * p + 4)
                for g in range(G):
                    for k in range(HP):
                        last = product(QK[:, g * F:(g + 1) * F], lambda i, k: ot[i][:, k, g, :], lambda j, k: wo[j][:, k, :], k,
                                       first=g == 0 and k == 0, last=k == HP - 1)
                last.then_inc(s["wo_done"], 1)

            def exponents(p):
                pe.wait_ge(s["xt3_lo"], p + 1)
                for k in range(FT):
                    product(O2[:, 0:256], lambda i, k: wj[i][:, k, :], lambda j, k: xt3[j][:, k].rearrange("p g n -> p (g n)"), k,
                            first=k == 0, last=k == FT - 1)
                for g in range(G):
                    for k in range(FT):
                        last = product(O2[:, 256 + g:257 + g], lambda i, k: xt3[i][:, k, g, :], lambda j, k: wi[j][:, k, :], k,
                                       last=k == FT - 1)
                last.then_inc(s["e3_done"], 1)

            def hop(dst, n, first=True):
                for g in range(G):
                    for k in range(FT):
                        last = product(dst[:, g * F:(g + 1) * F], lambda i, k: xt3[i][:, k, g, :], lambda j, k: wl[j][:, k, n, :], k,
                                       first=first and g == 0 and k == 0, last=k == FT - 1)
                return last

            def hops(p):
                pe.wait_ge(s["e_made"], p + 1)
                hop(O2, 1)
                for n in range(2):
                    pe.matmul(O3[:, :], ones16[:, :], bks[n][:, :].unsqueeze(1).to_broadcast([1, G, F]),
                              start=n == 0, stop=False, skip_group_check=True)
                hop(O3, 0, first=False)

            def transition_transposed(p):
                pe.wait_ge(s["tn_made"], p + 1)
                pe.wait_ge(s["hw2_made"], p + 1)
                for g in range(G):
                    last = pe.transpose(O1[:, g * P:(g + 1) * P], tn[:, g, :], ident[:, :])
                last.then_inc(s["mt_done"], 1)

            def diffuse(p, dst, src, ready, done):
                pe.wait_ge(ready, p + 1)
                for g in range(G):
                    last = pe.matmul(dst[:, g * F:(g + 1) * F], tt[:, g, :], src[:, g, :], start=False, stop=True,
                                     skip_group_check=True)
                last.then_inc(done, 1)

            def step(t, has01, has3):
                a, b, c = t + 1, t, t - 1
                transposes(b, x2, TP, s["x2_made"], s["xt2_done"])
                if has01:
                    transposes(a, x0, O1, s["x0_loaded"], s["x0t_done"], 16)
                    adjacency_t(a)
                project_qk(b, 0)
                project_v(b, 0)
                scores(b, 0)
                if has01:
                    aggregate0(a)
                    layer0_x(a)
                project_qk(b, 1)
                project_v(b, 1)
                scores(b, 1)
                if has01:
                    layer0_agg(a)
                if has3:
                    transposes(c, x3, O1, s["x3_made"], s["xt3_done"])
                attention_t(b, 0)
                project_qk(b, 2)
                apply_attention(b, 0)
                scores(b, 2)
                if has3:
                    exponents(c)
                    hop(O1, 2).then_inc(s["w2_done"], 1)
                attention_t(b, 1)
                if has01:
                    aggregate1(a)
                project_qk(b, 3)
                apply_attention(b, 1)
                scores(b, 3)
                if has01:
                    layer1(a)
                if has3:
                    hops(c)
                    transition_transposed(c)
                attention_t(b, 2)
                if has3:
                    diffuse(c, O2, hw2, s["tt_made"], s["t1_done"])
                apply_attention(b, 2)
                attention_t(b, 3)
                if has3:
                    diffuse(c, O3, u1, s["u1_made"], s["t0_done"])
                apply_attention(b, 3)
                project_out(b)

            transposes(0, x0, O1, s["x0_loaded"], s["x0t_done"], 16)
            adjacency_t(0)
            aggregate0(0)
            layer0_x(0)
            layer0_agg(0)
            aggregate1(0)
            layer1(0)
            schedule(pe, step)
            q = PAIRS - 1
            transposes(q, x3, O1, s["x3_made"], s["xt3_done"])
            exponents(q)
            hop(O1, 2).then_inc(s["w2_done"], 1)
            hops(q)
            transition_transposed(q)
            diffuse(q, O2, hw2, s["tt_made"], s["t1_done"])
            diffuse(q, O3, u1, s["u1_made"], s["t0_done"])


_INS = ["x", "adj", "nodemask", "L0_gnn_W", "L1_gnn_W", "L1_gnn_b", "L2_gnn_W_qkv", "L2_gnn_W_out", "L2_gnn_b_out",
        "L3_gnn_Wv", "L3_gnn_bv", "L3_gnn_aw", "L3_gnn_ab", "L3_gnn_Wk", "L3_gnn_bk"]


def kernel(**inputs):
    import numpy as _np
    import concourse.bacc as _bacc
    from concourse import mybir as _mybir
    from concourse.bass_utils import run_bass_kernel_spmd as _run

    nc = _bacc.Bacc("TRN2", target_bir_lowering=False, num_devices=1)
    arrays, args = {}, []
    for name in _INS:
        a = _np.ascontiguousarray(inputs[name])
        if a.dtype == _np.bool_:
            a = a.view(_np.uint8)
        arrays[f"in_{name}"] = a
        args.append(nc.dram_tensor(f"in_{name}", a.shape, _mybir.dt.from_np(a.dtype), kind="ExternalInput").ap())
    out = nc.dram_tensor("out_0", inputs["x"].shape, _mybir.dt.float32, kind="ExternalOutput").ap()
    build(nc, *args, out)
    r = _run(nc, [arrays], core_ids=[0])
    return r.results[0]["out_0"]
```

```python
import concourse.bass as bass
from concourse import mybir
from contextlib import ExitStack

F32 = mybir.dt.float32
F16 = mybir.dt.float16
BF16 = mybir.dt.bfloat16
U8 = mybir.dt.uint8
ALU = mybir.AluOpType
ACT = mybir.ActivationFunctionType
AX = mybir.AxisListType.X

P = 128
G = 2
F = 256
FT = F // P
HEADS = 8
DH = 64
HP = HEADS // 2
INNER = HEADS * DH
HOPS = 3
WS = 256.0
LAMBDA = 0.33
SCALE = DH ** -0.5
BIG = 1e30
LN_EPS = 1e-5
DEG_EPS = 1e-6
SUM_EPS = 1e-12

SEMS = """
ident_made weights_loaded consts_loaded setup_hi setup_lo setup_psum setup_moved bks_moved setup_dve setup_pool
x0_loaded adj0_loaded mask_loaded adj3_loaded out_stored
deg_summed deg_clamped deg_inverted adjn_made edges_counted dinv_made
x0t_done a0t_done xt0_hi xt0_lo adjnt_made at_made
ag_done agt_hi agt_lo l0_done relu0_made y0_made
x1_made y1_hi y1_lo ya_done yt_hi yt_lo h1_done z_made tanh_made y1b_made x2_made sdinv_made
mask_rows mask_tiles exp_adj_made c0_made c_rows c_made xt2_done xt2_hi xt2_lo xb_made
qk_done q_made k_made v_done v_made d_done negmax_made exps_made rsum_made pn_made attn_made
tr_done pt_made pv_done ot_hi ot_lo wo_done y2_made x3_made
xt3_done xt3_hi xt3_lo e3_done w2_done si_made e_made leaky_made expe_made m_made ssum_made rs_made tn_made
mt_done tt_hi tt_lo hw2_hi hw2_lo t1_done u1_hi u1_lo sidot_made t0_done relu3_made y3_made xo_made
bn0 bn1 bn2 bn3 aggr0 aggr1 aggr2 aggr3 vare0 vare1 vare2 vare3 rstd0 rstd1 rstd2 rstd3
""".split()


def build(nc, x, adj, nodemask, w0, w1, b1, wqkv, wout, bout, wv, bv, aw, ab, wk, bk, out):
    GRAPHS = x.shape[0]
    PAIRS = GRAPHS // G
    assert x.shape[1:] == (P, F) and GRAPHS % G == 0 and GRAPHS == P and PAIRS >= 4

    x_pair = x.rearrange("(t g) n f -> t n g f", g=G)
    adj_pair = adj.rearrange("(t g) n m -> t n g m", g=G)
    out_pair = out.rearrange("(t g) n f -> t n g f", g=G)
    mask_pair = nodemask.rearrange("(t g) n -> t (g n)", g=G)

    with ExitStack() as ctx:
        def sb(name, shape, dt=F32):
            return ctx.enter_context(nc.sbuf_tensor(name, shape, dt))

        s = {n: ctx.enter_context(nc.semaphore(n)) for n in SEMS}

        ident = sb("ident", [P, P])
        raw0 = sb("raw0", [P, FT, 2 * F])
        raw1 = sb("raw1", [P, FT, F])
        rawq = sb("rawq", [P, FT, 3 * INNER])
        rawo = sb("rawo", [P, HP, F])
        rawk = sb("rawk", [P, FT, HOPS, F])
        rawv = sb("rawv", [P, FT, F])
        wvt = sb("wvt", [P, FT, F])
        acol = sb("acol", [P, 2 * FT])
        asum = sb("asum", [P, FT])
        bvcol = sb("bvcol", [P, FT])
        bvrep = sb("bvrep", [P, FT, P])
        arep = sb("arep", [P, 2 * FT, P])
        abc = sb("abc", [P, 1])
        econst = sb("econst", [P, 1])
        b1bc = sb("b1bc", [P, F])
        bobc = sb("bobc", [P, F])
        bkrow = sb("bkrow", [1, HOPS, F])
        bksum = sb("bksum", [1, F])
        bksum2 = sb("bksum2", [1, F])
        epsln = sb("epsln", [P, G])
        mhalf = sb("mhalf", [P, G])
        mask8all = sb("mask8all", [P, P], U8)
        maskf = sb("maskf", [P, P])
        maskt = sb("maskt", [P, P])
        ones16 = sb("ones16", [2, P], F16)
        ident16 = sb("ident16", [P, P], F16)

        def pair_of_parts(name, shape):
            return sb(name + "_hi", shape, F16), sb(name + "_lo", shape, F16)

        w0t = pair_of_parts("w0t", [P, 2 * FT, F])
        w1p = pair_of_parts("w1p", [P, FT, F])
        wq = pair_of_parts("wq", [P, FT, HP, P])
        wkk = pair_of_parts("wkk", [P, FT, HP, P])
        wvv = pair_of_parts("wvv", [P, FT, INNER])
        wo = pair_of_parts("wo", [P, HP, F])
        wl = pair_of_parts("wl", [P, FT, HOPS, F])
        wj = pair_of_parts("wj", [P, FT, P])
        wirow = sb("wirow", [P, F])
        bks = pair_of_parts("bks", [1, F])
        bks2 = sb("bks2", [2, F], F16)

        x0 = sb("x0", [P, G, F])
        adj0 = sb("adj0", [P, G, P])
        deg = sb("deg", [P, G])
        degc = sb("degc", [P, G])
        rdeg = sb("rdeg", [P, G])
        adjn = sb("adjn", [P, G, P])
        edges = sb("edges", [P, G, P], F16)
        nedges = sb("nedges", [P, G])
        dinv = sb("dinv", [P, G])
        sdinv = sb("sdinv", [P, G])
        xt0 = pair_of_parts("xt0", [P, FT, G, P])
        adjnt = sb("adjnt", [P, G, P])
        at = sb("at", [P, G, P], F16)
        agt = pair_of_parts("agt", [P, FT, G, P])
        relu0 = sb("relu0", [P, G, F])
        y0 = sb("y0", [P, G, F])
        x1 = sb("x1", [P, G, F])
        y1 = pair_of_parts("y1", [P, G, F])
        yt = pair_of_parts("yt", [P, FT, G, P])
        z1 = sb("z1", [P, G, F])
        tanh1 = sb("tanh1", [P, G, F])
        y1b = sb("y1b", [P, G, F])
        x2 = sb("x2", [P, G, F])
        mask8 = sb("mask8", [P, G, P], U8)
        maskbc = sb("maskbc", [P, G, P])
        maskcol = sb("maskcol", [P, G])
        maskrow = sb("maskrow", [1, G, P], BF16)
        bigrow = sb("bigrow", [1, G, P], BF16)
        expadj = sb("expadj", [P, G, P])
        c0 = sb("c0", [P, G, P])
        crow = sb("crow", [P, G, P])
        c2 = sb("c2", [P, G, P])
        xt2 = pair_of_parts("xt2", [P, FT, G, P])
        xb = sb("xb", [P, G, F])
        qt = sb("qt", [P, 2, G, P])
        kt = sb("kt", [P, 2, G, 2, P])
        vv = sb("vv", [P, G, INNER])
        negmax = sb("negmax", [P, 2, G * 2])
        rowsum = sb("rowsum", [P, 2, G * 2])
        rrow = sb("rrow", [P, 2, G * 2])
        probs = sb("probs", [P, 2, G * 2, P])
        pn = sb("pn", [P, 2, G * 2, P])
        attn = sb("attn", [P, 2, G, 2, P])
        pt = sb("pt", [P, G, 2, P])
        ot = pair_of_parts("ot", [P, HP, G, P])
        y2 = sb("y2", [P, G, F])
        x3 = sb("x3", [P, G, F])
        adj3 = sb("adj3", [P, G, P])
        xt3 = pair_of_parts("xt3", [P, FT, G, P])
        sidot = sb("sidot", [P, G])
        sijunk = sb("sijunk", [P, G, F])
        si = sb("si", [P, G])
        ee = sb("ee", [P, G, P])
        leaky = sb("leaky", [P, G, P])
        expe = sb("expe", [P, G, P])
        mm = sb("mm", [P, G, P])
        ssum = sb("ssum", [P, G])
        ssume = sb("ssume", [P, G])
        rs = sb("rs", [P, G])
        tn = sb("tn", [P, G, P])
        tt = pair_of_parts("tt", [P, G, P])
        hw2 = pair_of_parts("hw2", [P, G, F])
        u1 = pair_of_parts("u1", [P, G, F])
        relu3 = sb("relu3", [P, G, F])
        y3 = sb("y3", [P, G, F])
        xo = sb("xo", [P, G, F])
        stats = sb("stats", [P, 4, G, 6])
        mv = sb("mv", [P, 4, G, 2])
        vare = sb("vare", [P, 4, G])
        rstd = sb("rstd", [P, 4, G])

        def bank(name):
            return ctx.enter_context(nc.psum_tensor(name, [P, 512], F32))

        QK, VB, DA, DB, TP, O1, O2, O3 = (bank(n) for n in ("QK", "VB", "DA", "DB", "TP", "O1", "O2", "O3"))
        SC = (DA, DB)

        EDGES_T = O2[:, 256:384].bitcast(F16).rearrange("p (g n) -> p g n", g=G)

        def v4(b):
            return b[:, :].rearrange("p (a g n) -> p a g n", a=2, g=G)

        def v3(b):
            return b[:, :].rearrange("p (g f) -> p g f", g=G)

        def half(b, k):
            return b[:, k * 256:(k + 1) * 256].rearrange("p (g n) -> p g n", g=G)

        def hold(eng, sem, n):
            if not (isinstance(n, int) and n <= 0):
                eng.wait_ge(sem, n)

        def stand_alone(eng):
            eng.wait_ge(s["ident_made"], 1)

        qkv_head = rawq[:, :, :].rearrange("p t (h s d) -> p t h s d", s=3, d=DH)

        AHEAD, BEHIND = 2, 1

        def go(stage, p, *which):
            if not isinstance(p, int) or 0 <= p < PAIRS:
                stage(p, *which)

        def run(eng, step, ahead=AHEAD):
            for t in range(-ahead, BEHIND + 1):
                step(t)
            with eng.Fori(BEHIND + 1, PAIRS - ahead) as t:
                step(t)
            for t in range(PAIRS - ahead, PAIRS + BEHIND):
                step(t)

        block = ctx.enter_context(nc.Block())

        @block.sync
        def _(sp):
            for dst, src in ((raw0[:, :, :], w0.rearrange("(t p) f -> p t f", p=P)),
                             (raw1[:, :, :], w1.rearrange("(t p) f -> p t f", p=P)),
                             (rawq[:, :, :], wqkv.rearrange("(t p) f -> p t f", p=P)),
                             (rawo[:, :, :], wout.rearrange("(t p) f -> p t f", p=P)),
                             (rawv[:, :, :], wv.rearrange("(t p) f -> p t f", p=P))):
                sp.dma_start(dst, src).then_inc(s["weights_loaded"], 16)
            for k in range(HOPS):
                sp.dma_start(rawk[:, :, k, :], wk[k].rearrange("(t p) f -> p t f", p=P)).then_inc(s["weights_loaded"], 16)

            def load_x0(p):
                stand_alone(sp)
                hold(sp, s["ag_done"], p)
                hold(sp, s["y0_made"], p)
                sp.dma_start(x0[:, :, :], x_pair[p]).then_inc(s["x0_loaded"], 16)

            def load_adj0(p):
                stand_alone(sp)
                hold(sp, s["a0t_done"], p)
                hold(sp, s["edges_counted"], p)
                hold(sp, s["c0_made"], p)
                sp.dma_start(adj0[:, :, :], adj_pair[p]).then_inc(s["adj0_loaded"], 16)

            def load_adj3(p):
                stand_alone(sp)
                hold(sp, s["m_made"], p)
                sp.dma_start(adj3[:, :, :], adj_pair[p]).then_inc(s["adj3_loaded"], 16)

            def store(p):
                stand_alone(sp)
                sp.wait_ge(s["xo_made"], p + 1)
                sp.dma_start(out_pair[p], xo[:, :, :]).then_inc(s["out_stored"], 16)

            def step(t):
                go(load_x0, t + 3)
                go(load_adj3, t + 1)
                go(load_adj0, t + 3)
                go(store, t - 1)
            run(sp, step, ahead=AHEAD + 1)
            sp.wait_ge(s["out_stored"], 16 * PAIRS)

        @block.gpsimd
        def _(pool):
            pool.memset(ident[:, :], 0.0).then_inc(s["setup_pool"], 1)
            pool.wait_ge(s["setup_pool"], 1)
            pool.affine_select(out=ident[:, :], in_=ident[:, :], compare_op=ALU.not_equal, fill=1.0,
                               base=0, pattern=[[-1, P]], channel_multiplier=1).then_inc(s["ident_made"], 1)
            pool.memset(epsln[:, :], LN_EPS).then_inc(s["setup_pool"], 1)
            pool.memset(mhalf[:, :], -0.5).then_inc(s["setup_pool"], 1)
            pool.memset(ones16[:, :], 1.0).then_inc(s["setup_pool"], 1)
            pool.memset(kt[:, :, :, :, :], 0.0).then_inc(s["setup_pool"], 1)
            pool.wait_ge(s["ident_made"], 1)
            pool.tensor_copy(ident16[:, :], ident[:, :]).then_inc(s["setup_pool"], 1)
            pool.wait_ge(s["setup_pool"], 6)
            pool.wait_ge(s["consts_loaded"], 16 * 7)

            def x2_plus_bias(p):
                pool.wait_ge(s["x2_made"], p + 1)
                hold(pool, s["y2_made"], p)
                pool.tensor_tensor(xb[:, :, :], x2[:, :, :], bobc[:, :].unsqueeze(1).to_broadcast([P, G, F]),
                                   ALU.add).then_inc(s["xb_made"], 1)

            def distance(p):
                pool.wait_ge(s["exp_adj_made"], p + 1)
                hold(pool, s["c_rows"], p)
                pool.tensor_tensor(c0[:, :, :], adj0[:, :, :], expadj[:, :, :], ALU.add).then_inc(s["c0_made"], 1)

            def inv_sqrt_degree(p):
                pool.wait_ge(s["edges_counted"], p + 1)
                hold(pool, s["z_made"], p)
                pool.tensor_tensor(dinv[:, :], nedges[:, :], mhalf[:, :], ALU.pow).then_inc(s["dinv_made"], 1)

            def residual(p, made, out_t, a, b, a_made, out_read):
                pool.wait_ge(a_made, p + 1)
                hold(pool, out_read, p)
                pool.tensor_tensor(out_t[:, :, :], a[:, :, :], b[:, :, :], ALU.add).then_inc(made, 1)

            def rstd_of(layer, p, aggr, vare_s, rstd_s):
                pool.wait_ge(aggr, p + 1)
                pool.tensor_tensor(vare[:, layer, :], mv[:, layer, :, 1], epsln[:, :], ALU.add).then_inc(vare_s, 1)
                pool.wait_ge(vare_s, p + 1)
                pool.tensor_tensor(rstd[:, layer, :], vare[:, layer, :], mhalf[:, :], ALU.pow).then_inc(rstd_s, 1)

            def residual0(p):
                pool.wait_ge(s["x0_loaded"], 16 * (p + 1))
                residual(p, s["y0_made"], y0, relu0, x0, s["relu0_made"], s["x1_made"])

            def add_c(p, h):
                pool.wait_ge(s["pn_made"], 4 * p + h + 1)
                if h == 0:
                    pool.wait_ge(s["c_made"], p + 1)
                hold(pool, s["tr_done"], 4 * p + h - 1)
                pool.tensor_tensor(attn[:, h % 2], pn[:, h % 2].rearrange("p (g e) n -> p g e n", g=G),
                                   c2[:, :, :].unsqueeze(2).to_broadcast([P, G, 2, P]), ALU.add).then_inc(s["attn_made"], 1)

            def residual1(p):
                residual(p, s["y1b_made"], y1b, tanh1, x1, s["tanh_made"], s["x2_made"])

            def residual3(p):
                residual(p, s["y3_made"], y3, relu3, x3, s["relu3_made"], s["xo_made"])

            def rstd0(p):
                rstd_of(0, p, s["aggr0"], s["vare0"], s["rstd0"])

            def rstd1(p):
                rstd_of(1, p, s["aggr1"], s["vare1"], s["rstd1"])

            def rstd2(p):
                rstd_of(2, p, s["aggr2"], s["vare2"], s["rstd2"])

            def rstd3(p):
                rstd_of(3, p, s["aggr3"], s["vare3"], s["rstd3"])

            def step(t):
                go(add_c, t, 2)
                go(x2_plus_bias, t)
                go(add_c, t, 3)
                go(residual1, t + 1)
                go(rstd1, t + 1)
                go(residual3, t - 1)
                go(rstd2, t)
                go(residual0, t + 2)
                go(inv_sqrt_degree, t + 2)
                go(rstd0, t + 2)
                go(add_c, t + 1, 0)
                go(distance, t + 2)
                go(rstd3, t - 1)
                go(add_c, t + 1, 1)
            run(pool, step)

        @block.scalar
        def _(act):
            act.dma_start(acol[:, :], aw.rearrange("(t p) o -> p (t o)", p=P), allow_slow_non_contiguous=True).then_inc(s["consts_loaded"], 16)
            act.dma_start(bvcol[:, :], bv.rearrange("(t p) -> p t", p=P), allow_slow_non_contiguous=True).then_inc(s["consts_loaded"], 16)
            act.dma_start(abc[:, :], ab.partition_broadcast(P)).then_inc(s["consts_loaded"], 16)
            act.dma_start(b1bc[:, :], b1.partition_broadcast(P)).then_inc(s["consts_loaded"], 16)
            act.dma_start(bobc[:, :], bout.partition_broadcast(P)).then_inc(s["consts_loaded"], 16)
            act.dma_start(bkrow[:, :, :], bk.unsqueeze(0)).then_inc(s["consts_loaded"], 16)
            act.dma_start(mask8all[:, :], nodemask).then_inc(s["consts_loaded"], 16)

            act.wait_ge(s["weights_loaded"], 16 * 8)
            act.activation(w1p[0][:, :, :], raw1[:, :, :], ACT.Copy, scale=WS).then_inc(s["setup_hi"], 1)
            act.activation(wo[0][:, :, :], rawo[:, :, :], ACT.Copy, scale=WS).then_inc(s["setup_hi"], 1)
            act.activation(wl[0][:, :, :, :], rawk[:, :, :, :], ACT.Copy, scale=WS).then_inc(s["setup_hi"], 1)
            for k in range(FT):
                for part, w in ((0, wq), (1, wkk)):
                    act.activation(w[0][:, k, :, :].rearrange("p h (e d) -> p (h e) d", e=2),
                                   qkv_head[:, k, :, part, :], ACT.Copy, scale=WS).then_inc(s["setup_hi"], 1)
                act.activation(wvv[0][:, k, :].rearrange("p (h d) -> p h d", h=HEADS),
                               qkv_head[:, k, :, 2, :], ACT.Copy, scale=WS).then_inc(s["setup_hi"], 1)
            act.wait_ge(s["setup_psum"], 1)
            act.activation(w0t[0][:, 0:2, :], v3(DA), ACT.Copy, scale=WS).then_inc(s["setup_hi"], 1)
            act.activation(w0t[0][:, 2:4, :], v3(DB), ACT.Copy, scale=WS).then_inc(s["setup_hi"], 1)
            act.wait_ge(s["setup_psum"], 4)
            act.activation(wj[0][:, :, :], half(O2, 0), ACT.Copy, scale=WS).then_inc(s["setup_hi"], 1)
            act.wait_ge(s["setup_dve"], 4)
            act.activation(bks[0][:, :], bksum2[:, :], ACT.Copy, scale=WS).then_inc(s["setup_hi"], 1)

            def high(p, hi, src, done, made):
                act.wait_ge(done, p + 1)
                act.activation(hi[:, :, :, :], v4(src), ACT.Copy).then_inc(made, 1)

            def adjacency_moved(p):
                act.wait_ge(s["a0t_done"], p + 1)
                act.activation(adjnt[:, :, :], half(O2, 0), ACT.Copy).then_inc(s["adjnt_made"], 1)
                act.activation(at[:, :, :], EDGES_T, ACT.Copy).then_inc(s["at_made"], 1)

            def exp_adj(p):
                act.wait_ge(s["adj0_loaded"], 16 * (p + 1))
                hold(act, s["c0_made"], p)
                act.activation(expadj[:, :, :], adj0[:, :, :], ACT.Exp, scale=-1.0).then_inc(s["exp_adj_made"], 1)

            def relu_of(p, dst, src, done, made, read):
                act.wait_ge(done, p + 1)
                hold(act, read, p)
                act.activation(dst[:, :, :], v3(src), ACT.Relu, scale=1.0 / WS).then_inc(made, 1)

            def relu_0(p):
                relu_of(p, relu0, O3, s["l0_done"], s["relu0_made"], s["y0_made"])

            def relu_3(p):
                relu_of(p, relu3, O3, s["t0_done"], s["relu3_made"], s["y3_made"])

            def tanh_1(p):
                act.wait_ge(s["z_made"], p + 1)
                hold(act, s["y1b_made"], p)
                act.activation(tanh1[:, :, :], z1[:, :, :], ACT.Tanh).then_inc(s["tanh_made"], 1)

            def key(p, h):
                act.wait_ge(s["q_made"], 4 * p + h + 1)
                for e in range(2):
                    rows = slice(e * DH, (e + 1) * DH)
                    last = act.activation(kt[rows, h % 2, :, e, :], QK[rows, 256:512].rearrange("p (g n) -> p g n", g=G),
                                          ACT.Copy, scale=1.0 / WS)
                last.then_inc(s["k_made"], 1)

            def value(p, g):
                act.wait_ge(s["v_done"], 2 * p + g + 1)
                act.activation(vv[:, g, :], VB[:, :], ACT.Copy, scale=LAMBDA / WS).then_inc(s["v_made"], 1)

            def exps(p, h):
                act.wait_ge(s["negmax_made"], 4 * p + h + 1)
                hold(act, s["pn_made"], 4 * p + h - 1)
                for ge in range(2 * G):
                    last = act.activation(probs[:, h % 2, ge, :], SC[h % 2][:, ge * P:(ge + 1) * P], ACT.Exp,
                                          scale=-1.0, bias=negmax[:, h % 2, ge:ge + 1],
                                          accum_out=rowsum[:, h % 2, ge:ge + 1])
                last.then_inc(s["exps_made"], 1)

            def attn_moved(p, h):
                act.wait_ge(s["tr_done"], 4 * p + h + 1)
                act.activation(pt[:, :, :, :], v4(TP), ACT.Copy).then_inc(s["pt_made"], 1)

            def out_high(p, h):
                act.wait_ge(s["pv_done"], 4 * p + h + 1)
                act.activation(ot[0][:, h], half(TP, 0), ACT.Copy).then_inc(s["ot_hi"], 1)

            def hop2_high(p):
                act.wait_ge(s["w2_done"], p + 1)
                act.activation(hw2[0][:, :, :], v3(O1), ACT.Copy, scale=1.0 / WS).then_inc(s["hw2_hi"], 1)

            def exp_e(p):
                act.wait_ge(s["leaky_made"], p + 1)
                hold(act, s["m_made"], p)
                act.activation(expe[:, :, :], leaky[:, :, :], ACT.Exp).then_inc(s["expe_made"], 1)

            def transition_high(p):
                act.wait_ge(s["mt_done"], p + 1)
                act.activation(tt[0][:, :, :], half(O1, 0), ACT.Copy).then_inc(s["tt_hi"], 1)

            def hop1_high(p):
                act.wait_ge(s["t1_done"], p + 1)
                act.activation(u1[0][:, :, :], v3(O2), ACT.Copy, scale=1.0 / WS).then_inc(s["u1_hi"], 1)

            def load_mask(p):
                hold(act, s["mask_tiles"], p)
                act.dma_start(mask8[:, :, :].rearrange("p g n -> p (g n)"),
                              mask_pair[p].partition_broadcast(P)).then_inc(s["mask_loaded"], 16)

            def masks(p):
                act.wait_ge(s["mask_loaded"], 16 * (p + 1))
                hold(act, s["d_done"], 4 * p)
                hold(act, s["q_made"], 4 * p)
                hold(act, s["c_made"], p)
                act.activation(maskrow[:, :, :], mask8[0:1, :, :], ACT.Copy)
                act.activation(bigrow[:, :, :], mask8[0:1, :, :], ACT.Copy, scale=-BIG, bias=BIG).then_inc(s["mask_rows"], 1)
                act.activation(maskcol[:, :], maskt[:, bass.ds(p * G, G)], ACT.Copy)
                act.activation(maskbc[:, :, :], mask8[:, :, :], ACT.Copy).then_inc(s["mask_tiles"], 1)

            def x0_high(p):
                high(p, xt0[0], O1, s["x0t_done"], s["xt0_hi"])

            def aggregate0_high(p):
                high(p, agt[0], O1, s["ag_done"], s["agt_hi"])

            def aggregate1_high(p):
                high(p, yt[0], VB, s["ya_done"], s["yt_hi"])

            def x2_high(p):
                high(p, xt2[0], TP, s["xt2_done"], s["xt2_hi"])

            def x3_high(p):
                high(p, xt3[0], O1, s["xt3_done"], s["xt3_hi"])

            def step(t):
                go(transition_high, t - 1)
                go(attn_moved, t, 1)
                go(exps, t, 3)
                go(out_high, t, 1)
                go(masks, t + 1)
                go(attn_moved, t, 2)
                go(hop1_high, t - 1)
                go(load_mask, t + 2)
                go(tanh_1, t + 1)
                go(out_high, t, 2)
                go(x0_high, t + 2)
                go(attn_moved, t, 3)
                go(adjacency_moved, t + 2)
                go(relu_3, t - 1)
                go(out_high, t, 3)
                go(aggregate0_high, t + 2)
                go(x2_high, t + 1)
                go(relu_0, t + 2)
                go(key, t + 1, 0)
                go(x3_high, t)
                go(value, t + 1, 0)
                go(key, t + 1, 1)
                go(exps, t + 1, 0)
                go(value, t + 1, 1)
                go(exp_e, t)
                go(key, t + 1, 2)
                go(exp_adj, t + 2)
                go(hop2_high, t)
                go(exps, t + 1, 1)
                go(attn_moved, t + 1, 0)
                go(key, t + 1, 3)
                go(aggregate1_high, t + 2)
                go(out_high, t + 1, 0)
                go(exps, t + 1, 2)
            act.wait_ge(s["setup_pool"], 5)
            act.wait_ge(s["setup_moved"], 3)
            act.wait_ge(s["setup_lo"], 15)
            act.dma_start(bks2[0:1, :], bks[0][:, :]).then_inc(s["bks_moved"], 16)
            act.dma_start(bks2[1:2, :], bks[1][:, :]).then_inc(s["bks_moved"], 16)
            run(act, step)

        @block.vector
        def _(dve):
            def low(w_lo, src, w_hi):
                return dve.scalar_tensor_tensor(out=w_lo, in0=src, scalar=WS, in1=w_hi,
                                                op0=ALU.mult, op1=ALU.subtract).then_inc(s["setup_lo"], 1)

            dve.wait_ge(s["consts_loaded"], 16 * 7)
            dve.tensor_copy(maskf[:, :], mask8all[:, :]).then_inc(s["setup_dve"], 1)
            dve.tensor_copy(bvrep[:, :, :], bvcol[:, :].unsqueeze(2).to_broadcast([P, FT, P])).then_inc(s["setup_moved"], 1)
            dve.tensor_copy(arep[:, :, :], acol[:, :].unsqueeze(2).to_broadcast([P, 2 * FT, P])).then_inc(s["setup_dve"], 1)
            dve.tensor_tensor(bksum[:, :], bkrow[:, 0, :], bkrow[:, 1, :], ALU.add).then_inc(s["setup_dve"], 1)
            dve.wait_ge(s["setup_dve"], 3)
            dve.tensor_tensor(bksum2[:, :], bksum[:, :], bkrow[:, 2, :], ALU.add).then_inc(s["setup_dve"], 1)
            dve.tensor_tensor(asum[:, :], acol[:, 0:FT], acol[:, FT:2 * FT], ALU.add).then_inc(s["setup_dve"], 1)
            dve.wait_ge(s["setup_psum"], 2)
            dve.tensor_copy(wvt[:, :, :], v3(O1)).then_inc(s["setup_moved"], 1)
            dve.wait_ge(s["setup_psum"], 3)
            dve.tensor_copy(maskt[:, :], O3[:, 0:P]).then_inc(s["setup_moved"], 1)
            dve.wait_ge(s["setup_hi"], 9)
            low(w1p[1][:, :, :], raw1[:, :, :], w1p[0][:, :, :])
            low(wo[1][:, :, :], rawo[:, :, :], wo[0][:, :, :])
            low(wl[1][:, :, :, :].rearrange("p t k f -> p (t k f)"), rawk[:, :, :, :].rearrange("p t k f -> p (t k f)"),
                wl[0][:, :, :, :].rearrange("p t k f -> p (t k f)"))
            for k in range(FT):
                for part, w in ((0, wq), (1, wkk)):
                    low(w[1][:, k, :, :].rearrange("p h (e d) -> p (h e) d", e=2), qkv_head[:, k, :, part, :],
                        w[0][:, k, :, :].rearrange("p h (e d) -> p (h e) d", e=2))
                low(wvv[1][:, k, :].rearrange("p (h d) -> p h d", h=HEADS), qkv_head[:, k, :, 2, :],
                    wvv[0][:, k, :].rearrange("p (h d) -> p h d", h=HEADS))
            dve.wait_ge(s["setup_hi"], 11)
            low(w0t[1][:, 0:2, :], v3(DA), w0t[0][:, 0:2, :])
            low(w0t[1][:, 2:4, :], v3(DB), w0t[0][:, 2:4, :])
            dve.wait_ge(s["setup_hi"], 13)
            low(wj[1][:, :, :], half(O2, 0), wj[0][:, :, :])
            dve.tensor_copy(wirow[:, :], O3[:, 128:384]).then_inc(s["setup_lo"], 1)
            dve.tensor_scalar(econst[:, :], O3[:, 384:385], abc[:, :], None, ALU.add).then_inc(s["setup_lo"], 1)
            low(bks[1][:, :], bksum2[:, :], bks[0][:, :])

            def rest(p, lo, hi, src, hi_made, made):
                dve.wait_ge(hi_made, p + 1)
                dve.tensor_tensor(lo[:, :, :, :], v4(src), hi[:, :, :, :], ALU.subtract).then_inc(made, 1)

            def normalised_adjacency(p):
                dve.wait_ge(s["adj0_loaded"], 16 * (p + 1))
                dve.tensor_reduce(deg[:, :], adj0[:, :, :], AX, ALU.add).then_inc(s["deg_summed"], 1)
                hold(dve, s["dinv_made"], p)
                for g in range(G):
                    last = dve.scalar_tensor_tensor(out=edges[:, g, :], in0=adj0[:, g, :], scalar=0.0, in1=ident[:, :],
                                                    op0=ALU.not_equal, op1=ALU.max, accum_out=nedges[:, g:g + 1])
                last.then_inc(s["edges_counted"], 1)
                dve.wait_ge(s["deg_summed"], p + 1)
                dve.tensor_scalar(degc[:, :], deg[:, :], DEG_EPS, None, ALU.max).then_inc(s["deg_clamped"], 1)
                dve.wait_ge(s["deg_clamped"], p + 1)
                dve.reciprocal(rdeg[:, :], degc[:, :]).then_inc(s["deg_inverted"], 1)
                dve.wait_ge(s["deg_inverted"], p + 1)
                hold(dve, s["a0t_done"], p)
                for g in range(G):
                    last = dve.tensor_scalar(adjn[:, g, :], adj0[:, g, :], rdeg[:, g:g + 1], None, ALU.mult)
                last.then_inc(s["adjn_made"], 1)

            def norm_stats(layer, p, src, made, bn, aggr):
                dve.wait_ge(made, p + 1)
                for g in range(G):
                    last = dve.bn_stats(stats[:, layer, g, :], src[:, g, :])
                last.then_inc(bn, 1)
                stand_alone(dve)
                dve.wait_ge(bn, p + 1)
                for g in range(G):
                    last = dve.bn_aggr(mv[:, layer, g, :], stats[:, layer, g, :])
                last.then_inc(aggr, 1)

            def norm_apply(layer, p, dst, src, rstd_s, made):
                dve.wait_ge(rstd_s, p + 1)
                for g in range(G):
                    last = dve.tensor_scalar(dst[:, g, :], src[:, g, :], mv[:, layer, g, 0:1], rstd[:, layer, g:g + 1],
                                             ALU.subtract, ALU.mult)
                last.then_inc(made, 1)

            def ln0_stats(p):
                norm_stats(0, p, y0, s["y0_made"], s["bn0"], s["aggr0"])

            def ln0_apply(p):
                hold(dve, s["y1b_made"], p)
                norm_apply(0, p, x1, y0, s["rstd0"], s["x1_made"])
                dve.wait_ge(s["dinv_made"], p + 1)
                dve.wait_ge(s["x1_made"], p + 1)
                dve.tensor_scalar(sdinv[:, :], dinv[:, :], 1.0 / WS, None, ALU.mult).then_inc(s["sdinv_made"], 1)
                for g in range(G):
                    last = dve.tensor_scalar(y1[0][:, g, :], x1[:, g, :], dinv[:, g:g + 1], None, ALU.mult)
                last.then_inc(s["y1_hi"], 1)
                dve.wait_ge(s["y1_hi"], p + 1)
                for g in range(G):
                    last = dve.scalar_tensor_tensor(out=y1[1][:, g, :], in0=x1[:, g, :], scalar=dinv[:, g:g + 1],
                                                    in1=y1[0][:, g, :], op0=ALU.mult, op1=ALU.subtract)
                last.then_inc(s["y1_lo"], 1)

            def before_tanh(p):
                dve.wait_ge(s["h1_done"], p + 1)
                dve.wait_ge(s["sdinv_made"], p + 1)
                for g in range(G):
                    last = dve.scalar_tensor_tensor(out=z1[:, g, :], in0=VB[:, g * F:(g + 1) * F], scalar=sdinv[:, g:g + 1],
                                                    in1=b1bc[:, :], op0=ALU.mult, op1=ALU.add)
                last.then_inc(s["z_made"], 1)

            def ln1_stats(p):
                norm_stats(1, p, y1b, s["y1b_made"], s["bn1"], s["aggr1"])

            def ln1_apply(p):
                hold(dve, s["xb_made"], p)
                norm_apply(1, p, x2, y1b, s["rstd1"], s["x2_made"])

            def masked_c(p):
                dve.wait_ge(s["mask_tiles"], p + 1)
                dve.wait_ge(s["c0_made"], p + 1)
                for g in range(G):
                    last = dve.tensor_scalar(crow[:, g, :], c0[:, g, :], maskcol[:, g:g + 1], None, ALU.mult)
                last.then_inc(s["c_rows"], 1)
                dve.wait_ge(s["c_rows"], p + 1)
                hold(dve, s["attn_made"], 4 * p)
                dve.tensor_tensor(c2[:, :, :], crow[:, :, :], maskbc[:, :, :], ALU.mult).then_inc(s["c_made"], 1)

            def query(p, h):
                dve.wait_ge(s["qk_done"], 4 * p + h + 1)
                if h == 0:
                    dve.wait_ge(s["mask_tiles"], p + 1)
                dve.scalar_tensor_tensor(out=qt[:, h % 2], in0=half(QK, 0), scalar=-SCALE / WS, in1=maskbc[:, :, :],
                                         op0=ALU.mult, op1=ALU.mult).then_inc(s["q_made"], 1)

            def minus_max(p, h):
                dve.wait_ge(s["d_done"], 4 * p + h + 1)
                dve.tensor_reduce(negmax[:, h % 2, :], SC[h % 2][:, :].rearrange("p (a n) -> p a n", n=P), AX,
                                  ALU.min).then_inc(s["negmax_made"], 1)

            def normalise(p, h):
                dve.wait_ge(s["exps_made"], 4 * p + h + 1)
                dve.reciprocal(rrow[:, h % 2, :], rowsum[:, h % 2, :]).then_inc(s["rsum_made"], 1)
                dve.wait_ge(s["rsum_made"], 4 * p + h + 1)
                hold(dve, s["attn_made"], 4 * p + h - 1)
                dve.tensor_tensor(pn[:, h % 2], probs[:, h % 2],
                                  rrow[:, h % 2, :].unsqueeze(2).to_broadcast([P, 2 * G, P]), ALU.mult).then_inc(s["pn_made"], 1)

            def out_low(p, h):
                dve.wait_ge(s["ot_hi"], 4 * p + h + 1)
                dve.tensor_tensor(ot[1][:, h], half(TP, 0), ot[0][:, h], ALU.subtract).then_inc(s["ot_lo"], 1)

            def residual2(p):
                dve.wait_ge(s["wo_done"], p + 1)
                dve.wait_ge(s["xb_made"], p + 1)
                dve.scalar_tensor_tensor(out=y2[:, :, :], in0=v3(QK), scalar=1.0 / WS, in1=xb[:, :, :],
                                         op0=ALU.mult, op1=ALU.add).then_inc(s["y2_made"], 1)

            def ln2_stats(p):
                norm_stats(2, p, y2, s["y2_made"], s["bn2"], s["aggr2"])

            def ln2_apply(p):
                hold(dve, s["y3_made"], p)
                norm_apply(2, p, x3, y2, s["rstd2"], s["x3_made"])

            def own_exponent(p):
                dve.wait_ge(s["x3_made"], p + 1)
                for g in range(G):
                    last = dve.scalar_tensor_tensor(out=sijunk[:, g, :], in0=x3[:, g, :], scalar=1.0, in1=wirow[:, :],
                                                    op0=ALU.mult, op1=ALU.mult, accum_out=sidot[:, g:g + 1])
                last.then_inc(s["sidot_made"], 1)
                dve.wait_ge(s["sidot_made"], p + 1)
                dve.tensor_scalar(si[:, :], sidot[:, :], econst[:, :], None, ALU.add).then_inc(s["si_made"], 1)

            def exponent(p):
                dve.wait_ge(s["e3_done"], p + 1)
                dve.wait_ge(s["si_made"], p + 1)
                for g in range(G):
                    last = dve.tensor_scalar(ee[:, g, :], O2[:, g * P:(g + 1) * P], 1.0 / WS, si[:, g:g + 1], ALU.mult, ALU.add)
                last.then_inc(s["e_made"], 1)
                dve.wait_ge(s["e_made"], p + 1)
                dve.scalar_tensor_tensor(out=leaky[:, :, :], in0=ee[:, :, :], scalar=0.2, in1=ee[:, :, :],
                                         op0=ALU.mult, op1=ALU.max).then_inc(s["leaky_made"], 1)

            def transition(p):
                dve.wait_ge(s["expe_made"], p + 1)
                dve.wait_ge(s["adj3_loaded"], 16 * (p + 1))
                for g in range(G):
                    last = dve.scalar_tensor_tensor(out=mm[:, g, :], in0=expe[:, g, :], scalar=1.0, in1=adj3[:, g, :],
                                                    op0=ALU.mult, op1=ALU.mult, accum_out=ssum[:, g:g + 1])
                last.then_inc(s["m_made"], 1)
                dve.wait_ge(s["m_made"], p + 1)
                dve.tensor_scalar(ssume[:, :], ssum[:, :], SUM_EPS, None, ALU.add).then_inc(s["ssum_made"], 1)
                dve.wait_ge(s["ssum_made"], p + 1)
                dve.reciprocal(rs[:, :], ssume[:, :]).then_inc(s["rs_made"], 1)
                dve.wait_ge(s["rs_made"], p + 1)
                hold(dve, s["mt_done"], p)
                for g in range(G):
                    last = dve.tensor_scalar(tn[:, g, :], mm[:, g, :], rs[:, g:g + 1], WS, ALU.mult, ALU.mult)
                last.then_inc(s["tn_made"], 1)

            def transition_low(p):
                dve.wait_ge(s["tt_hi"], p + 1)
                dve.tensor_tensor(tt[1][:, :, :], half(O1, 0), tt[0][:, :, :], ALU.subtract).then_inc(s["tt_lo"], 1)

            def hop_low(p, src, dst, hi_made, made):
                dve.wait_ge(hi_made, p + 1)
                dve.scalar_tensor_tensor(out=dst[1][:, :, :], in0=v3(src), scalar=1.0 / WS, in1=dst[0][:, :, :],
                                         op0=ALU.mult, op1=ALU.subtract).then_inc(made, 1)

            def ln3_stats(p):
                norm_stats(3, p, y3, s["y3_made"], s["bn3"], s["aggr3"])

            def ln3_apply(p):
                hold(dve, s["out_stored"], 16 * p)
                norm_apply(3, p, xo, y3, s["rstd3"], s["xo_made"])

            def x0_low(p):
                rest(p, xt0[1], xt0[0], O1, s["xt0_hi"], s["xt0_lo"])

            def aggregate0_low(p):
                rest(p, agt[1], agt[0], O1, s["agt_hi"], s["agt_lo"])

            def aggregate1_low(p):
                rest(p, yt[1], yt[0], VB, s["yt_hi"], s["yt_lo"])

            def x2_low(p):
                rest(p, xt2[1], xt2[0], TP, s["xt2_hi"], s["xt2_lo"])

            def x3_low(p):
                rest(p, xt3[1], xt3[0], O1, s["xt3_hi"], s["xt3_lo"])

            def hop2_low(p):
                hop_low(p, O1, hw2, s["hw2_hi"], s["hw2_lo"])

            def hop1_low(p):
                hop_low(p, O2, u1, s["u1_hi"], s["u1_lo"])

            def step(t):
                go(transition_low, t - 1)
                go(out_low, t, 1)
                go(normalise, t, 3)
                go(before_tanh, t + 1)
                go(normalised_adjacency, t + 2)
                go(out_low, t, 2)
                go(hop1_low, t - 1)
                go(x0_low, t + 2)
                go(ln1_stats, t + 1)
                go(out_low, t, 3)
                go(ln1_apply, t + 1)
                go(aggregate0_low, t + 2)
                go(ln3_stats, t - 1)
                go(masked_c, t + 1)
                go(x2_low, t + 1)
                go(residual2, t)
                go(ln2_stats, t)
                go(query, t + 1, 0)
                go(ln2_apply, t)
                go(own_exponent, t)
                go(ln0_stats, t + 2)
                go(x3_low, t)
                go(minus_max, t + 1, 0)
                go(query, t + 1, 1)
                go(ln0_apply, t + 2)
                go(exponent, t)
                go(query, t + 1, 2)
                go(normalise, t + 1, 0)
                go(minus_max, t + 1, 1)
                go(transition, t)
                go(hop2_low, t)
                go(query, t + 1, 3)
                go(normalise, t + 1, 1)
                go(minus_max, t + 1, 2)
                go(out_low, t + 1, 0)
                go(aggregate1_low, t + 2)
                go(minus_max, t + 1, 3)
                go(normalise, t + 1, 2)
                go(ln3_apply, t - 1)
            dve.wait_ge(s["ident_made"], 1)
            run(dve, step)

        @block.tensor
        def _(pe):
            def product(dst, lhs, rhs, k, first=False, last=False):
                for n, (i, j) in enumerate(((0, 0), (0, 1), (1, 0))):
                    mm_ = pe.matmul(dst, lhs(i, k), rhs(j, k), start=first and n == 0, stop=last and n == 2,
                                    skip_group_check=True)
                return mm_

            pe.wait_ge(s["ident_made"], 1)
            pe.wait_ge(s["weights_loaded"], 16 * 8)
            for c in range(2 * FT):
                for o in range(FT):
                    dst = (DA, DB)[c // 2][:, (c % 2) * F + o * P:(c % 2) * F + (o + 1) * P]
                    last = pe.transpose(dst, raw0[:, o, c * P:(c + 1) * P], ident[:, :])
            last.then_inc(s["setup_psum"], 1)
            for d in range(FT):
                for f in range(FT):
                    last = pe.transpose(O1[:, d * F + f * P:d * F + (f + 1) * P], rawv[:, f, d * P:(d + 1) * P], ident[:, :])
            last.then_inc(s["setup_psum"], 1)
            pe.wait_ge(s["setup_dve"], 5)
            pe.transpose(O3[:, 0:P], maskf[:, :], ident[:, :]).then_inc(s["setup_psum"], 1)
            pe.wait_ge(s["setup_moved"], 3)
            for f in range(FT):
                for d in range(FT):
                    pe.matmul(O2[:, f * P:(f + 1) * P], wvt[:, d, f * P:(f + 1) * P], arep[:, d, :],
                              start=f == 0 and d == 0, stop=d == 1, skip_group_check=True)
            for d in range(FT):
                pe.matmul(O3[:, 128:384], arep[:, FT + d, :], wvt[:, d, :], start=d == 0, stop=d == 1, skip_group_check=True)
            for d in range(FT):
                last = pe.matmul(O3[:, 384:385], bvrep[:, d, :], asum[:, d:d + 1], start=False, stop=d == 1,
                                 skip_group_check=True)
            last.then_inc(s["setup_psum"], 1)
            pe.wait_ge(s["setup_lo"], 15)
            pe.wait_ge(s["setup_pool"], 6)

            def from_later(p, later, earlier):
                if isinstance(p, int) and p + AHEAD >= PAIRS:
                    hold(pe, earlier, p)
                else:
                    pe.wait_ge(later, p + AHEAD + 1)

            def from_earlier(p, earlier, before):
                if isinstance(p, int) and p <= AHEAD:
                    hold(pe, before, p)
                else:
                    pe.wait_ge(earlier, p - AHEAD)

            def transposes(p, src, dst, ready, done, n=1):
                pe.wait_ge(ready, n * (p + 1))
                for k in range(FT):
                    for g in range(G):
                        last = pe.transpose(dst[:, (k * G + g) * P:(k * G + g + 1) * P], src[:, g, k * P:(k + 1) * P], ident[:, :])
                last.then_inc(done, 1)

            def adjacency_transposed(p):
                pe.wait_ge(s["adjn_made"], p + 1)
                from_earlier(p, s["u1_lo"], s["at_made"])
                for g in range(G):
                    pe.transpose(O2[:, g * P:(g + 1) * P], adjn[:, g, :], ident[:, :])
                for g in range(G):
                    last = pe.transpose(EDGES_T[:, g, :], edges[:, g, :], ident16[:, :])
                last.then_inc(s["a0t_done"], 1)

            def nodes_by_weights(p, dst, lhs, rhs, ks, first, wgt0=0):
                for g in range(G):
                    for k in ks:
                        last = product(dst[:, g * F:(g + 1) * F], lambda i, k: lhs[i][:, k, g, :],
                                       lambda j, k: rhs[j][:, wgt0 + k, :], k,
                                       first=first and g == 0 and k == ks[0], last=k == ks[-1])
                return last

            def aggregate0(p):
                pe.wait_ge(s["adjnt_made"], p + 1)
                pe.wait_ge(s["xt0_lo"], p + 1)
                for k in range(FT):
                    for g in range(G):
                        last = pe.matmul(O1[:, (k * G + g) * P:(k * G + g + 1) * P], x0[:, g, k * P:(k + 1) * P], adjnt[:, g, :],
                                         start=k == 0 and g == 0, stop=True, skip_group_check=True)
                last.then_inc(s["ag_done"], 1)

            def layer0_x(p):
                pe.wait_ge(s["xt0_lo"], p + 1)
                from_earlier(p, s["relu3_made"], s["relu0_made"])
                nodes_by_weights(p, O3, xt0, w0t, range(FT), True)

            def layer0_agg(p):
                pe.wait_ge(s["agt_lo"], p + 1)
                nodes_by_weights(p, O3, agt, w0t, range(FT), False, wgt0=FT).then_inc(s["l0_done"], 1)

            def aggregate1(p):
                pe.wait_ge(s["y1_lo"], p + 1)
                pe.wait_ge(s["at_made"], p + 1)
                hold(pe, s["v_made"], 2 * p)
                for k in range(FT):
                    for g in range(G):
                        for n in range(2):
                            last = pe.matmul(VB[:, (k * G + g) * P:(k * G + g + 1) * P], y1[n][:, g, k * P:(k + 1) * P],
                                             at[:, g, :], start=k == 0 and g == 0 and n == 0, stop=n == 1,
                                             skip_group_check=True)
                last.then_inc(s["ya_done"], 1)

            def layer1(p):
                pe.wait_ge(s["yt_lo"], p + 1)
                nodes_by_weights(p, VB, yt, w1p, range(FT), True).then_inc(s["h1_done"], 1)

            def project_qk(p, h):
                if h == 0:
                    pe.wait_ge(s["xt2_lo"], p + 1)
                    hold(pe, s["y2_made"], p)
                else:
                    pe.wait_ge(s["k_made"], 4 * p + h)
                for part, w in enumerate((wq, wkk)):
                    for k in range(FT):
                        last = product(QK[:, part * 256:(part + 1) * 256], lambda i, k: w[i][:, k, h, :],
                                       lambda j, k: xt2[j][:, k].rearrange("p g n -> p (g n)"), k,
                                       first=part == 0 and k == 0, last=k == FT - 1)
                last.then_inc(s["qk_done"], 1)

            def project_v(p, g):
                if g == 0:
                    pe.wait_ge(s["xt2_lo"], p + 1)
                    pe.wait_ge(s["z_made"], p + 1)
                else:
                    pe.wait_ge(s["v_made"], 2 * p + 1)
                for k in range(FT):
                    last = product(VB[:, :], lambda i, k: xt2[i][:, k, g, :], lambda j, k: wvv[j][:, k, :], k,
                                   first=k == 0, last=k == FT - 1)
                last.then_inc(s["v_done"], 1)

            def scores(p, h):
                if h == 0:
                    pe.wait_ge(s["mask_rows"], p + 1)
                pe.wait_ge(s["k_made"], 4 * p + h + 1)
                hold(pe, s["exps_made"], 4 * p + h - 1)
                bank_ = SC[h % 2]
                for g in range(G):
                    pe.matmul(bank_[:, g * 256:(g + 1) * 256], maskrow[0:1, g, :],
                              bigrow[0:1, g:g + 1, :].to_broadcast([1, 2, P]), start=g == 0, stop=False, skip_group_check=True)
                for g in range(G):
                    last = pe.matmul(bank_[:, g * 256:(g + 1) * 256], qt[:, h % 2, g, :],
                                     kt[:, h % 2, g].rearrange("p e n -> p (e n)"), start=False, stop=True,
                                     skip_group_check=True)
                last.then_inc(s["d_done"], 1)

            def attention_transposed(p, h):
                pe.wait_ge(s["attn_made"], 4 * p + h + 1)
                if h > 0:
                    pe.wait_ge(s["ot_lo"], 4 * p + h)
                for g in range(G):
                    for e in range(2):
                        last = pe.transpose(TP[:, (2 * g + e) * P:(2 * g + e + 1) * P], attn[:, h % 2, g, e, :], ident[:, :])
                last.then_inc(s["tr_done"], 1)

            def apply_attention(p, h):
                pe.wait_ge(s["pt_made"], 4 * p + h + 1)
                if h == 0:
                    pe.wait_ge(s["v_made"], 2 * p + 2)
                for g in range(G):
                    for e in range(2):
                        head = 2 * h + e
                        last = pe.matmul(TP[e * DH:(e + 1) * DH, g * P:(g + 1) * P], vv[:, g, head * DH:(head + 1) * DH],
                                         pt[:, g, e, :], start=True, stop=True, skip_group_check=True)
                last.then_inc(s["pv_done"], 1)

            def project_out(p):
                pe.wait_ge(s["ot_lo"], 4 * p + 4)
                pe.wait_ge(s["k_made"], 4 * p + 4)
                for g in range(G):
                    for k in range(HP):
                        last = product(QK[:, g * F:(g + 1) * F], lambda i, k: ot[i][:, k, g, :], lambda j, k: wo[j][:, k, :], k,
                                       first=g == 0 and k == 0, last=k == HP - 1)
                last.then_inc(s["wo_done"], 1)

            def exponents(p):
                pe.wait_ge(s["xt3_lo"], p + 1)
                from_later(p, s["at_made"], s["u1_lo"])
                for k in range(FT):
                    last = product(O2[:, 0:256], lambda i, k: wj[i][:, k, :], lambda j, k: xt3[j][:, k].rearrange("p g n -> p (g n)"), k,
                            first=k == 0, last=k == FT - 1)
                last.then_inc(s["e3_done"], 1)

            def hop(dst, n, first=True):
                for g in range(G):
                    for k in range(FT):
                        last = product(dst[:, g * F:(g + 1) * F], lambda i, k: xt3[i][:, k, g, :], lambda j, k: wl[j][:, k, n, :], k,
                                       first=first and g == 0 and k == 0, last=k == FT - 1)
                return last

            def hop1_product(p):
                pe.wait_ge(s["e_made"], p + 1)
                hop(O2, 1)

            def hop0_product(p):
                from_later(p, s["relu0_made"], s["relu3_made"])
                pe.wait_ge(s["bks_moved"], 32)
                pe.matmul(O3[:, :], ones16[:, :], bks2[:, :].unsqueeze(1).to_broadcast([2, G, F]),
                          start=True, stop=False, skip_group_check=True)
                hop(O3, 0, first=False)

            def transition_transposed(p):
                pe.wait_ge(s["tn_made"], p + 1)
                pe.wait_ge(s["hw2_lo"], p + 1)
                for g in range(G):
                    last = pe.transpose(O1[:, g * P:(g + 1) * P], tn[:, g, :], ident[:, :])
                last.then_inc(s["mt_done"], 1)

            def diffuse(p, dst, src, ready, done):
                pe.wait_ge(ready, p + 1)
                for g in range(G):
                    last = product(dst[:, g * F:(g + 1) * F], lambda i, k: tt[i][:, g, :], lambda j, k: src[j][:, g, :], 0,
                                   last=True)
                last.then_inc(done, 1)

            def x0_transposed(p):
                from_earlier(p, s["tt_lo"], s["agt_lo"])
                transposes(p, x0, O1, s["x0_loaded"], s["x0t_done"], 16)

            def x2_transposed(p):
                hold(pe, s["ot_lo"], 4 * p)
                transposes(p, x2, TP, s["x2_made"], s["xt2_done"])

            def x3_transposed(p):
                from_later(p, s["agt_lo"], s["tt_lo"])
                transposes(p, x3, O1, s["x3_made"], s["xt3_done"])

            def hop2_product(p):
                pe.wait_ge(s["xt3_lo"], p + 1)
                hop(O1, 2).then_inc(s["w2_done"], 1)

            def diffuse1(p):
                pe.wait_ge(s["tt_lo"], p + 1)
                diffuse(p, O2, hw2, s["hw2_lo"], s["t1_done"])

            def diffuse0(p):
                diffuse(p, O3, u1, s["u1_lo"], s["t0_done"])

            def step(t):
                go(apply_attention, t, 1)
                go(layer1, t + 1)
                go(attention_transposed, t, 2)
                go(diffuse1, t - 1)
                go(x0_transposed, t + 2)
                go(apply_attention, t, 2)
                go(hop0_product, t - 1)
                go(attention_transposed, t, 3)
                go(adjacency_transposed, t + 2)
                go(diffuse0, t - 1)
                go(apply_attention, t, 3)
                go(aggregate0, t + 2)
                go(layer0_x, t + 2)
                go(x2_transposed, t + 1)
                go(project_out, t)
                go(layer0_agg, t + 2)
                go(project_qk, t + 1, 0)
                go(project_v, t + 1, 0)
                go(x3_transposed, t)
                go(scores, t + 1, 0)
                go(project_qk, t + 1, 1)
                go(exponents, t)
                go(project_v, t + 1, 1)
                go(project_qk, t + 1, 2)
                go(scores, t + 1, 1)
                go(hop2_product, t)
                go(project_qk, t + 1, 3)
                go(attention_transposed, t + 1, 0)
                go(scores, t + 1, 2)
                go(aggregate1, t + 2)
                go(apply_attention, t + 1, 0)
                go(transition_transposed, t)
                go(scores, t + 1, 3)
                go(attention_transposed, t + 1, 1)
                go(hop1_product, t)
            run(pe, step)


_INS = ["x", "adj", "nodemask", "L0_gnn_W", "L1_gnn_W", "L1_gnn_b", "L2_gnn_W_qkv", "L2_gnn_W_out", "L2_gnn_b_out",
        "L3_gnn_Wv", "L3_gnn_bv", "L3_gnn_aw", "L3_gnn_ab", "L3_gnn_Wk", "L3_gnn_bk"]


def kernel(**inputs):
    import numpy as _np
    import concourse.bacc as _bacc
    from concourse import mybir as _mybir
    from concourse.bass_utils import run_bass_kernel_spmd as _run

    nc = _bacc.Bacc("TRN2", target_bir_lowering=False, num_devices=1)
    arrays, args = {}, []
    for name in _INS:
        a = _np.ascontiguousarray(inputs[name])
        if a.dtype == _np.bool_:
            a = a.view(_np.uint8)
        arrays[f"in_{name}"] = a
        args.append(nc.dram_tensor(f"in_{name}", a.shape, _mybir.dt.from_np(a.dtype), kind="ExternalInput").ap())
    out = nc.dram_tensor("out_0", inputs["x"].shape, _mybir.dt.float32, kind="ExternalOutput").ap()
    build(nc, *args, out)
    r = _run(nc, [arrays], core_ids=[0])
    return r.results[0]["out_0"]
```

```python
import concourse.bass as bass
from concourse import mybir
from contextlib import ExitStack

F32 = mybir.dt.float32
F16 = mybir.dt.float16
BF16 = mybir.dt.bfloat16
U8 = mybir.dt.uint8
ALU = mybir.AluOpType
ACT = mybir.ActivationFunctionType
AX = mybir.AxisListType.X

P = 128
G = 2
F = 256
FT = F // P
HEADS = 8
DH = 64
HP = HEADS // 2
UNITS = HP
INNER = HEADS * DH
HOPS = 3
WS = 256.0
LAMBDA = 0.33
SCALE = DH ** -0.5
BIG = 1e30
LN_EPS = 1e-5
DEG_EPS = 1e-6
SUM_EPS = 1e-12

SEMS = """
ident_made raw0_loaded rawv_loaded raw1_loaded rawo_loaded rawq_loaded rawk_loaded consts_loaded setup_hi setup_lo setup_psum setup_moved setup_dve setup_pool
x0_loaded adj0_loaded mask_loaded adj3_loaded out_stored
deg_summed deg_clamped deg_inverted adjn_made edges_counted dinv_made
x0t_done a0t_done xt0_hi xt0_lo adjnt_made at_made
ag_done agt_hi agt_lo l0_done relu0_made y0_made
x1_made y1_hi y1_lo ya_done yt_hi yt_lo h1_done z_made tanh_made y1b_made x2_made sdinv_made
mask_rows mask_tiles exp_adj_made c0_made c_rows c_made xt2_done xt2_hi xt2_lo xb_made
qk_done q_made k_made v_done v_made d_done negmax_made exps_made rsum_made pn_made attn_made
tr_done pt_made pv_done ot_hi ot_lo wo_done y2_made x3_made
xt3_done xt3_hi xt3_lo e3_done w2_done si_made sj_made sj_hi sj_lo e_made leaky_made expe_made m_made ssum_made rs_made tn_made
mt_done tt_hi tt_lo hw2_hi hw2_lo t1_done u1_hi u1_lo sidot_made t0_done hb_made relu3_made y3_made xo_made
bn0 bn1 bn2 bn3 aggr0 aggr1 aggr2 aggr3 vare0 vare1 vare2 vare3 rstd0 rstd1 rstd2 rstd3
""".split()


def build(nc, x, adj, nodemask, w0, w1, b1, wqkv, wout, bout, wv, bv, aw, ab, wk, bk, out):
    GRAPHS = x.shape[0]
    PAIRS = GRAPHS // G
    assert x.shape[1:] == (P, F) and GRAPHS % G == 0 and GRAPHS == P and PAIRS >= 4

    x_pair = x.rearrange("(t g) n f -> t n g f", g=G)
    adj_pair = adj.rearrange("(t g) n m -> t n g m", g=G)
    out_pair = out.rearrange("(t g) n f -> t n g f", g=G)
    mask_pair = nodemask.rearrange("(t g) n -> t (g n)", g=G)

    with ExitStack() as ctx:
        def sb(name, shape, dt=F32):
            return ctx.enter_context(nc.sbuf_tensor(name, shape, dt))

        s = {n: ctx.enter_context(nc.semaphore(n)) for n in SEMS}

        ident = sb("ident", [P, P])
        raw0 = sb("raw0", [P, FT, 2 * F])
        raw1 = sb("raw1", [P, FT, F])
        rawq = sb("rawq", [P, FT, 3 * INNER])
        rawo = sb("rawo", [P, HP, F])
        rawk = sb("rawk", [P, FT, HOPS, F])
        rawv = sb("rawv", [P, FT, F])
        wvt = sb("wvt", [P, FT, F])
        acol = sb("acol", [P, 2 * FT])
        asum = sb("asum", [P, FT])
        bvcol = sb("bvcol", [P, FT])
        bvrep = sb("bvrep", [P, FT, P])
        arep = sb("arep", [P, 2 * FT, P])
        abc = sb("abc", [P, 1])
        econst = sb("econst", [P, 1])
        b1bc = sb("b1bc", [P, F])
        bobc = sb("bobc", [P, F])
        bkbc = sb("bkbc", [P, HOPS, F])
        bksum = sb("bksum", [P, F])
        bksum2 = sb("bksum2", [P, F])
        epsln = sb("epsln", [P, G])
        mhalf = sb("mhalf", [P, G])
        mask8all = sb("mask8all", [P, P], U8)
        maskf = sb("maskf", [P, P])
        maskt = sb("maskt", [P, P])
        ident16 = sb("ident16", [P, P], F16)

        def pair_of_parts(name, shape):
            return sb(name + "_hi", shape, F16), sb(name + "_lo", shape, F16)

        w0t = pair_of_parts("w0t", [P, 2 * FT, F])
        w1p = pair_of_parts("w1p", [P, FT, F])
        wq = pair_of_parts("wq", [P, FT, HP, P])
        wkk = pair_of_parts("wkk", [P, FT, HP, P])
        wvv = pair_of_parts("wvv", [P, FT, INNER])
        wo = pair_of_parts("wo", [P, HP, F])
        wl = pair_of_parts("wl", [P, FT, HOPS, F])
        wjrow = sb("wjrow", [P, F])
        wirow = sb("wirow", [P, F])

        x0 = sb("x0", [P, G, F])
        adj0 = sb("adj0", [P, G, P])
        deg = sb("deg", [P, G])
        degc = sb("degc", [P, G])
        rdeg = sb("rdeg", [P, G])
        adjn = sb("adjn", [P, G, P])
        edges = sb("edges", [P, G, P], F16)
        nedges = sb("nedges", [P, G])
        dinv = sb("dinv", [P, G])
        sdinv = sb("sdinv", [P, G])
        xt0 = pair_of_parts("xt0", [P, FT, G, P])
        adjnt = sb("adjnt", [P, G, P])
        at = sb("at", [P, G, P], F16)
        agt = pair_of_parts("agt", [P, FT, G, P])
        relu0 = sb("relu0", [P, G, F])
        y0 = sb("y0", [P, G, F])
        x1 = sb("x1", [P, G, F])
        y1 = pair_of_parts("y1", [P, G, F])
        yt = pair_of_parts("yt", [P, FT, G, P])
        z1 = sb("z1", [P, G, F])
        tanh1 = sb("tanh1", [P, G, F])
        y1b = sb("y1b", [P, G, F])
        x2 = sb("x2", [P, G, F])
        mask8 = sb("mask8", [P, G, P], U8)
        maskbc = sb("maskbc", [P, G, P])
        maskcol = sb("maskcol", [P, G])
        maskrow = sb("maskrow", [P, G, P], BF16)
        bigrow = sb("bigrow", [P, G, P], BF16)
        expadj = sb("expadj", [P, G, P])
        c0 = sb("c0", [P, G, P])
        crow = sb("crow", [P, G, P])
        c2 = sb("c2", [P, G, P])
        xt2 = pair_of_parts("xt2", [P, FT, G, P])
        xb = sb("xb", [P, G, F])
        qt = sb("qt", [P, HP, G, P])
        kt = sb("kt", [P, HP, G, P])
        vv = sb("vv", [P, G, INNER])
        negmax = sb("negmax", [P, 2, G * 2])
        rowsum = sb("rowsum", [P, 2, G * 2])
        rrow = sb("rrow", [P, 2, G * 2])
        probs = sb("probs", [P, 2, G * 2, P])
        pn = sb("pn", [P, 2, G * 2, P])
        attn = sb("attn", [P, 2, G, 2, P])
        pt = sb("pt", [P, G, 2, P])
        ot = pair_of_parts("ot", [P, HP, G, P])
        y2 = sb("y2", [P, G, F])
        x3 = sb("x3", [P, G, F])
        adj3 = sb("adj3", [P, G, P])
        xt3 = pair_of_parts("xt3", [P, FT, G, P])
        sidot = sb("sidot", [P, G])
        sj = sb("sj", [P, G])
        sjrep = pair_of_parts("sjrep", [P, G, P])
        sjjunk = sb("sjjunk", [P, G, F])
        sijunk = sb("sijunk", [P, G, F])
        si = sb("si", [P, G])
        ee = sb("ee", [P, G, P])
        leaky = sb("leaky", [P, G, P])
        expe = sb("expe", [P, G, P])
        mm = sb("mm", [P, G, P])
        ssum = sb("ssum", [P, G])
        ssume = sb("ssume", [P, G])
        rs = sb("rs", [P, G])
        tn = sb("tn", [P, G, P])
        tt = pair_of_parts("tt", [P, G, P])
        hw2 = pair_of_parts("hw2", [P, G, F])
        u1 = pair_of_parts("u1", [P, G, F])
        hb = sb("hb", [P, G, F])
        relu3 = sb("relu3", [P, G, F])
        y3 = sb("y3", [P, G, F])
        xo = sb("xo", [P, G, F])
        stats = sb("stats", [P, 4, G, 6])
        mv = sb("mv", [P, 4, G, 2])
        vare = sb("vare", [P, 4, G])
        rstd = sb("rstd", [P, 4, G])

        def bank(name):
            return ctx.enter_context(nc.psum_tensor(name, [P, 512], F32))

        QK, VB, DA, DB, TP, O1, O2, O3 = (bank(n) for n in ("QK", "VB", "DA", "DB", "TP", "O1", "O2", "O3"))
        SC = (DA, DB)

        EDGES_T = O2[:, 256:384].bitcast(F16).rearrange("p (g n) -> p g n", g=G)

        def v4(b):
            return b[:, :].rearrange("p (a g n) -> p a g n", a=2, g=G)

        def v3(b):
            return b[:, :].rearrange("p (g f) -> p g f", g=G)

        def half(b, k):
            return b[:, k * 256:(k + 1) * 256].rearrange("p (g n) -> p g n", g=G)

        def hold(eng, sem, n):
            if not (isinstance(n, int) and n <= 0):
                eng.wait_ge(sem, n)

        def stand_alone(eng):
            eng.wait_ge(s["ident_made"], 1)

        qkv_head = rawq[:, :, :].rearrange("p t (h s d) -> p t h s d", s=3, d=DH)

        AHEAD, BEHIND = 2, 1

        def go(stage, p, *which):
            if not isinstance(p, int) or 0 <= p < PAIRS:
                stage(p, *which)

        def run(eng, step, ahead=AHEAD):
            for t in range(-ahead, BEHIND + 1):
                step(t)
            with eng.Fori(BEHIND + 1, PAIRS - ahead) as t:
                step(t)
            for t in range(PAIRS - ahead, PAIRS + BEHIND):
                step(t)

        block = ctx.enter_context(nc.Block())

        @block.sync
        def _(sp):
            sp.dma_start(raw0[:, :, :], w0.rearrange("(t p) f -> p t f", p=P)).then_inc(s["raw0_loaded"], 16)
            sp.dma_start(rawv[:, :, :], wv.rearrange("(t p) f -> p t f", p=P)).then_inc(s["rawv_loaded"], 16)
            sp.dma_start(raw1[:, :, :], w1.rearrange("(t p) f -> p t f", p=P)).then_inc(s["raw1_loaded"], 16)
            unit_rows = wout.rearrange("(j l e d) f -> l j d e f", j=2, l=2, e=2)
            for l in range(2):
                for j in range(2):
                    sp.dma_start(rawo[l * DH:(l + 1) * DH, 2 * j:2 * j + 2, :], unit_rows[l, j]).then_inc(s["rawo_loaded"], 16)
            sp.dma_start(rawq[:, :, :], wqkv.rearrange("(t p) f -> p t f", p=P)).then_inc(s["rawq_loaded"], 16)
            for k in range(HOPS):
                sp.dma_start(rawk[:, :, k, :], wk[k].rearrange("(t p) f -> p t f", p=P)).then_inc(s["rawk_loaded"], 16)

            def load_x0(p):
                stand_alone(sp)
                hold(sp, s["ag_done"], p)
                hold(sp, s["y0_made"], p)
                sp.dma_start(x0[:, :, :], x_pair[p]).then_inc(s["x0_loaded"], 16)

            def load_adj0(p):
                stand_alone(sp)
                hold(sp, s["a0t_done"], p)
                hold(sp, s["edges_counted"], p)
                hold(sp, s["c0_made"], p)
                sp.dma_start(adj0[:, :, :], adj_pair[p]).then_inc(s["adj0_loaded"], 16)

            def load_adj3(p):
                stand_alone(sp)
                hold(sp, s["m_made"], p)
                sp.dma_start(adj3[:, :, :], adj_pair[p]).then_inc(s["adj3_loaded"], 16)

            def store(p):
                stand_alone(sp)
                sp.wait_ge(s["xo_made"], p + 1)
                sp.dma_start(out_pair[p], xo[:, :, :]).then_inc(s["out_stored"], 16)

            def step(t):
                go(load_adj3, t)
                go(load_adj0, t + 3)
                go(load_x0, t + 3)
                go(store, t - 1)
            run(sp, step, ahead=AHEAD + 1)
            sp.wait_ge(s["out_stored"], 16 * PAIRS)

        @block.gpsimd
        def _(pool):
            pool.memset(ident[:, :], 0.0).then_inc(s["setup_pool"], 1)
            pool.wait_ge(s["setup_pool"], 1)
            pool.affine_select(out=ident[:, :], in_=ident[:, :], compare_op=ALU.not_equal, fill=1.0,
                               base=0, pattern=[[-1, P]], channel_multiplier=1).then_inc(s["ident_made"], 1)
            pool.memset(epsln[:, :], LN_EPS).then_inc(s["setup_pool"], 1)
            pool.memset(mhalf[:, :], -0.5).then_inc(s["setup_pool"], 1)
            pool.wait_ge(s["ident_made"], 1)
            pool.tensor_copy(ident16[:, :], ident[:, :]).then_inc(s["setup_pool"], 1)
            pool.wait_ge(s["setup_pool"], 4)
            pool.wait_ge(s["consts_loaded"], 16 * 7)

            def x2_plus_bias(p):
                pool.wait_ge(s["x2_made"], p + 1)
                hold(pool, s["y2_made"], p)
                pool.tensor_tensor(xb[:, :, :], x2[:, :, :], bobc[:, :].unsqueeze(1).to_broadcast([P, G, F]),
                                   ALU.add).then_inc(s["xb_made"], 1)

            def distance(p):
                pool.wait_ge(s["exp_adj_made"], p + 1)
                hold(pool, s["c_rows"], p)
                pool.tensor_tensor(c0[:, :, :], adj0[:, :, :], expadj[:, :, :], ALU.add).then_inc(s["c0_made"], 1)

            def inv_sqrt_degree(p):
                pool.wait_ge(s["edges_counted"], p + 1)
                hold(pool, s["z_made"], p)
                pool.tensor_tensor(dinv[:, :], nedges[:, :], mhalf[:, :], ALU.pow).then_inc(s["dinv_made"], 1)

            def residual(p, made, out_t, a, b, a_made, out_read):
                pool.wait_ge(a_made, p + 1)
                hold(pool, out_read, p)
                pool.tensor_tensor(out_t[:, :, :], a[:, :, :], b[:, :, :], ALU.add).then_inc(made, 1)

            def rstd_of(layer, p, aggr, vare_s, rstd_s):
                pool.wait_ge(aggr, p + 1)
                pool.tensor_tensor(vare[:, layer, :], mv[:, layer, :, 1], epsln[:, :], ALU.add).then_inc(vare_s, 1)
                pool.wait_ge(vare_s, p + 1)
                pool.tensor_tensor(rstd[:, layer, :], vare[:, layer, :], mhalf[:, :], ALU.pow).then_inc(rstd_s, 1)

            def residual0(p):
                pool.wait_ge(s["x0_loaded"], 16 * (p + 1))
                residual(p, s["y0_made"], y0, relu0, x0, s["relu0_made"], s["x1_made"])

            def add_c(p, u):
                pool.wait_ge(s["pn_made"], 4 * p + u + 1)
                if u == 0:
                    pool.wait_ge(s["c_made"], p + 1)
                hold(pool, s["tr_done"], 4 * p + u - 1)
                pool.tensor_tensor(attn[:, u % 2], pn[:, u % 2].rearrange("p (g l) n -> p g l n", g=G),
                                   c2[:, :, :].unsqueeze(2).to_broadcast([P, G, 2, P]), ALU.add).then_inc(s["attn_made"], 1)

            def residual1(p):
                residual(p, s["y1b_made"], y1b, tanh1, x1, s["tanh_made"], s["x2_made"])

            def residual3(p):
                residual(p, s["y3_made"], y3, relu3, x3, s["relu3_made"], s["xo_made"])

            def rstd0(p):
                rstd_of(0, p, s["aggr0"], s["vare0"], s["rstd0"])

            def rstd1(p):
                rstd_of(1, p, s["aggr1"], s["vare1"], s["rstd1"])

            def rstd2(p):
                rstd_of(2, p, s["aggr2"], s["vare2"], s["rstd2"])

            def rstd3(p):
                rstd_of(3, p, s["aggr3"], s["vare3"], s["rstd3"])

            def step(t):
                go(x2_plus_bias, t)
                go(add_c, t, 1)
                go(add_c, t, 2)
                go(add_c, t, 3)
                go(residual1, t + 1)
                go(rstd1, t + 1)
                go(distance, t + 2)
                go(residual3, t - 1)
                go(rstd2, t)
                go(residual0, t + 2)
                go(inv_sqrt_degree, t + 2)
                go(rstd3, t - 1)
                go(rstd0, t + 2)
                go(add_c, t + 1, 0)
            run(pool, step)

        @block.scalar
        def _(act):
            act.dma_start(acol[:, :], aw.rearrange("(t p) o -> p (t o)", p=P), allow_slow_non_contiguous=True).then_inc(s["consts_loaded"], 16)
            act.dma_start(bvcol[:, :], bv.rearrange("(t p) -> p t", p=P), allow_slow_non_contiguous=True).then_inc(s["consts_loaded"], 16)
            act.dma_start(abc[:, :], ab.partition_broadcast(P)).then_inc(s["consts_loaded"], 16)
            act.dma_start(b1bc[:, :], b1.partition_broadcast(P)).then_inc(s["consts_loaded"], 16)
            act.dma_start(bobc[:, :], bout.partition_broadcast(P)).then_inc(s["consts_loaded"], 16)
            act.dma_start(bkbc[:, :, :], bk.partition_broadcast(P)).then_inc(s["consts_loaded"], 16)
            act.dma_start(mask8all[:, :], nodemask).then_inc(s["consts_loaded"], 16)

            act.wait_ge(s["raw1_loaded"], 16)
            act.activation(w1p[0][:, :, :], raw1[:, :, :], ACT.Copy, scale=WS).then_inc(s["setup_hi"], 1)
            act.wait_ge(s["rawo_loaded"], 16 * 4)
            act.activation(wo[0][:, :, :], rawo[:, :, :], ACT.Copy, scale=WS).then_inc(s["setup_hi"], 1)
            act.wait_ge(s["rawq_loaded"], 16)
            for k in range(FT):
                for part, w in ((0, wq), (1, wkk)):
                    act.activation(w[0][:, k, :, :].rearrange("p h (e d) -> p (h e) d", e=2),
                                   qkv_head[:, k, :, part, :], ACT.Copy, scale=WS).then_inc(s["setup_hi"], 1)
                act.activation(wvv[0][:, k, :].rearrange("p (h d) -> p h d", h=HEADS),
                               qkv_head[:, k, :, 2, :], ACT.Copy, scale=WS).then_inc(s["setup_hi"], 1)
            act.wait_ge(s["rawk_loaded"], 16 * HOPS)
            act.activation(wl[0][:, :, :, :], rawk[:, :, :, :], ACT.Copy, scale=WS).then_inc(s["setup_hi"], 1)
            act.wait_ge(s["setup_psum"], 1)
            act.activation(w0t[0][:, 0:2, :], v3(DA), ACT.Copy, scale=WS).then_inc(s["setup_hi"], 1)
            act.activation(w0t[0][:, 2:4, :], v3(DB), ACT.Copy, scale=WS).then_inc(s["setup_hi"], 1)

            def high(p, hi, src, done, made):
                act.wait_ge(done, p + 1)
                act.activation(hi[:, :, :, :], v4(src), ACT.Copy).then_inc(made, 1)

            def adjacency_moved(p):
                act.wait_ge(s["a0t_done"], p + 1)
                act.activation(adjnt[:, :, :], half(O2, 0), ACT.Copy).then_inc(s["adjnt_made"], 1)
                act.activation(at[:, :, :], EDGES_T, ACT.Copy).then_inc(s["at_made"], 1)

            def exp_adj(p):
                act.wait_ge(s["adj0_loaded"], 16 * (p + 1))
                hold(act, s["c0_made"], p)
                act.activation(expadj[:, :, :], adj0[:, :, :], ACT.Exp, scale=-1.0).then_inc(s["exp_adj_made"], 1)

            def relu_0(p):
                act.wait_ge(s["l0_done"], p + 1)
                hold(act, s["y0_made"], p)
                act.activation(relu0[:, :, :], v3(O3), ACT.Relu, scale=1.0 / WS).then_inc(s["relu0_made"], 1)

            def relu_3(p):
                act.wait_ge(s["hb_made"], p + 1)
                hold(act, s["y3_made"], p)
                act.activation(relu3[:, :, :], hb[:, :, :], ACT.Relu).then_inc(s["relu3_made"], 1)

            def tanh_1(p):
                act.wait_ge(s["z_made"], p + 1)
                hold(act, s["y1b_made"], p)
                act.activation(tanh1[:, :, :], z1[:, :, :], ACT.Tanh).then_inc(s["tanh_made"], 1)

            def key(p, h):
                act.wait_ge(s["q_made"], 4 * p + h + 1)
                act.activation(kt[:, h], half(QK, 1), ACT.Copy, scale=1.0 / WS).then_inc(s["k_made"], 1)

            def value(p, g):
                act.wait_ge(s["v_done"], 2 * p + g + 1)
                act.activation(vv[:, g, :], VB[:, :], ACT.Copy, scale=LAMBDA / WS).then_inc(s["v_made"], 1)

            def exps(p, u):
                act.wait_ge(s["negmax_made"], 4 * p + u + 1)
                hold(act, s["pn_made"], 4 * p + u - 1)
                for ge in range(2 * G):
                    last = act.activation(probs[:, u % 2, ge, :], SC[u % 2][:, ge * P:(ge + 1) * P], ACT.Exp,
                                          scale=-1.0, bias=negmax[:, u % 2, ge:ge + 1],
                                          accum_out=rowsum[:, u % 2, ge:ge + 1])
                last.then_inc(s["exps_made"], 1)

            def attn_moved(p, u):
                act.wait_ge(s["tr_done"], 4 * p + u + 1)
                act.activation(pt[:, :, :, :], v4(TP), ACT.Copy).then_inc(s["pt_made"], 1)

            def out_high(p, u):
                act.wait_ge(s["pv_done"], 4 * p + u + 1)
                act.activation(ot[0][:, u], half(TP, 0), ACT.Copy).then_inc(s["ot_hi"], 1)

            def hop2_high(p):
                act.wait_ge(s["w2_done"], p + 1)
                act.activation(hw2[0][:, :, :], v3(O1), ACT.Copy, scale=1.0 / WS).then_inc(s["hw2_hi"], 1)

            def exp_e(p):
                act.wait_ge(s["leaky_made"], p + 1)
                hold(act, s["m_made"], p)
                act.activation(expe[:, :, :], leaky[:, :, :], ACT.Exp).then_inc(s["expe_made"], 1)

            def transition_high(p):
                act.wait_ge(s["mt_done"], p + 1)
                act.activation(tt[0][:, :, :], half(O1, 0), ACT.Copy).then_inc(s["tt_hi"], 1)

            def hop1_high(p):
                act.wait_ge(s["t1_done"], p + 1)
                act.activation(u1[0][:, :, :], v3(O2), ACT.Copy, scale=1.0 / WS).then_inc(s["u1_hi"], 1)

            def load_mask(p):
                hold(act, s["mask_tiles"], p)
                act.dma_start(mask8[:, :, :].rearrange("p g n -> p (g n)"),
                              mask_pair[p].partition_broadcast(P)).then_inc(s["mask_loaded"], 16)

            def masks(p):
                act.wait_ge(s["mask_loaded"], 16 * (p + 1))
                hold(act, s["d_done"], 2 * p)
                hold(act, s["q_made"], 4 * p)
                hold(act, s["c_made"], p)
                act.activation(maskrow[:, :, :], mask8[:, :, :], ACT.Copy)
                act.activation(bigrow[:, :, :], mask8[:, :, :], ACT.Copy, scale=-BIG, bias=BIG).then_inc(s["mask_rows"], 1)
                act.activation(maskcol[:, :], maskt[:, bass.ds(p * G, G)], ACT.Copy)
                act.activation(maskbc[:, :, :], mask8[:, :, :], ACT.Copy).then_inc(s["mask_tiles"], 1)

            def c_masked_rows(p):
                act.wait_ge(s["c0_made"], p + 1)
                act.wait_ge(s["mask_tiles"], p + 1)
                hold(act, s["c_made"], p)
                for g in range(G):
                    last = act.activation(crow[:, g, :], c0[:, g, :], ACT.Copy, scale=maskcol[:, g:g + 1])
                last.then_inc(s["c_rows"], 1)

            def adjacency_normalised(p):
                act.wait_ge(s["deg_inverted"], p + 1)
                hold(act, s["a0t_done"], p)
                for g in range(G):
                    last = act.activation(adjn[:, g, :], adj0[:, g, :], ACT.Copy, scale=rdeg[:, g:g + 1])
                last.then_inc(s["adjn_made"], 1)

            def y1_high(p):
                act.wait_ge(s["x1_made"], p + 1)
                act.wait_ge(s["dinv_made"], p + 1)
                hold(act, s["ya_done"], p)
                for g in range(G):
                    last = act.activation(y1[0][:, g, :], x1[:, g, :], ACT.Copy, scale=dinv[:, g:g + 1])
                last.then_inc(s["y1_hi"], 1)

            def share_high(p):
                act.wait_ge(s["sj_made"], p + 1)
                hold(act, s["e3_done"], p)
                act.activation(sjrep[0][:, :, :], sj[:, :].unsqueeze(2).to_broadcast([P, G, P]),
                               ACT.Copy).then_inc(s["sj_hi"], 1)

            def exponent(p):
                act.wait_ge(s["e3_done"], p + 1)
                act.wait_ge(s["si_made"], p + 1)
                hold(act, s["leaky_made"], p)
                for g in range(G):
                    last = act.activation(ee[:, g, :], O2[:, g * P:(g + 1) * P], ACT.Identity,
                                          bias=si[:, g:g + 1])
                last.then_inc(s["e_made"], 1)

            def x0_high(p):
                high(p, xt0[0], O1, s["x0t_done"], s["xt0_hi"])

            def aggregate0_high(p):
                high(p, agt[0], O1, s["ag_done"], s["agt_hi"])

            def aggregate1_high(p):
                high(p, yt[0], VB, s["ya_done"], s["yt_hi"])

            def x2_high(p):
                high(p, xt2[0], TP, s["xt2_done"], s["xt2_hi"])

            def x3_high(p):
                high(p, xt3[0], O1, s["xt3_done"], s["xt3_hi"])

            def step(t):
                go(out_high, t, 0)
                go(exps, t, 2)
                go(attn_moved, t, 1)
                go(transition_high, t - 1)
                go(aggregate1_high, t + 1)
                go(out_high, t, 1)
                go(exps, t, 3)
                go(attn_moved, t, 2)
                go(adjacency_normalised, t + 2)
                go(hop1_high, t - 1)
                go(out_high, t, 2)
                go(tanh_1, t + 1)
                go(x0_high, t + 2)
                go(exp_adj, t + 2)
                go(attn_moved, t, 3)
                go(adjacency_moved, t + 2)
                go(out_high, t, 3)
                go(aggregate0_high, t + 2)
                go(masks, t + 1)
                go(relu_3, t - 1)
                go(x2_high, t + 1)
                go(load_mask, t + 2)
                go(c_masked_rows, t + 1)
                go(key, t + 1, 0)
                go(relu_0, t + 2)
                go(key, t + 1, 1)
                go(value, t + 1, 0)
                go(share_high, t)
                go(x3_high, t)
                go(exponent, t)
                go(exps, t + 1, 0)
                go(key, t + 1, 2)
                go(exp_e, t)
                go(exps, t + 1, 1)
                go(y1_high, t + 2)
                go(key, t + 1, 3)
                go(attn_moved, t + 1, 0)
                go(hop2_high, t)
                go(value, t + 1, 1)
            act.wait_ge(s["setup_moved"], 3)
            run(act, step)

        @block.vector
        def _(dve):
            def low(w_lo, src, w_hi):
                return dve.scalar_tensor_tensor(out=w_lo, in0=src, scalar=WS, in1=w_hi,
                                                op0=ALU.mult, op1=ALU.subtract).then_inc(s["setup_lo"], 1)

            dve.wait_ge(s["consts_loaded"], 16 * 7)
            dve.tensor_copy(maskf[:, :], mask8all[:, :]).then_inc(s["setup_dve"], 1)
            dve.tensor_copy(bvrep[:, :, :], bvcol[:, :].unsqueeze(2).to_broadcast([P, FT, P])).then_inc(s["setup_moved"], 1)
            dve.tensor_copy(arep[:, :, :], acol[:, :].unsqueeze(2).to_broadcast([P, 2 * FT, P])).then_inc(s["setup_dve"], 1)
            dve.tensor_tensor(bksum[:, :], bkbc[:, 0, :], bkbc[:, 1, :], ALU.add).then_inc(s["setup_dve"], 1)
            dve.wait_ge(s["setup_dve"], 3)
            dve.tensor_tensor(bksum2[:, :], bksum[:, :], bkbc[:, 2, :], ALU.add).then_inc(s["setup_dve"], 1)
            dve.tensor_tensor(asum[:, :], acol[:, 0:FT], acol[:, FT:2 * FT], ALU.add).then_inc(s["setup_dve"], 1)
            dve.wait_ge(s["setup_psum"], 2)
            dve.tensor_copy(wvt[:, :, :], v3(O1)).then_inc(s["setup_moved"], 1)
            dve.wait_ge(s["setup_psum"], 3)
            dve.tensor_copy(maskt[:, :], O3[:, 0:P]).then_inc(s["setup_moved"], 1)
            dve.wait_ge(s["setup_hi"], 1)
            low(w1p[1][:, :, :], raw1[:, :, :], w1p[0][:, :, :])
            dve.wait_ge(s["setup_hi"], 2)
            low(wo[1][:, :, :], rawo[:, :, :], wo[0][:, :, :])
            for k in range(FT):
                dve.wait_ge(s["setup_hi"], 5 + 3 * k)
                for part, w in ((0, wq), (1, wkk)):
                    low(w[1][:, k, :, :].rearrange("p h (e d) -> p (h e) d", e=2), qkv_head[:, k, :, part, :],
                        w[0][:, k, :, :].rearrange("p h (e d) -> p (h e) d", e=2))
                low(wvv[1][:, k, :].rearrange("p (h d) -> p h d", h=HEADS), qkv_head[:, k, :, 2, :],
                    wvv[0][:, k, :].rearrange("p (h d) -> p h d", h=HEADS))
            dve.wait_ge(s["setup_hi"], 9)
            low(wl[1][:, :, :, :].rearrange("p t k f -> p (t k f)"), rawk[:, :, :, :].rearrange("p t k f -> p (t k f)"),
                wl[0][:, :, :, :].rearrange("p t k f -> p (t k f)"))
            dve.wait_ge(s["setup_hi"], 11)
            low(w0t[1][:, 0:2, :], v3(DA), w0t[0][:, 0:2, :])
            low(w0t[1][:, 2:4, :], v3(DB), w0t[0][:, 2:4, :])
            dve.wait_ge(s["setup_psum"], 4)
            dve.tensor_copy(wjrow[:, :], O2[:, 0:F]).then_inc(s["setup_lo"], 1)
            dve.tensor_copy(wirow[:, :], O3[:, 128:384]).then_inc(s["setup_lo"], 1)
            dve.tensor_scalar(econst[:, :], O3[:, 384:385], abc[:, :], None, ALU.add).then_inc(s["setup_lo"], 1)

            def rest(p, lo, hi, src, hi_made, made):
                dve.wait_ge(hi_made, p + 1)
                dve.tensor_tensor(lo[:, :, :, :], v4(src), hi[:, :, :, :], ALU.subtract).then_inc(made, 1)

            def degrees(p):
                dve.wait_ge(s["adj0_loaded"], 16 * (p + 1))
                dve.tensor_reduce(deg[:, :], adj0[:, :, :], AX, ALU.add).then_inc(s["deg_summed"], 1)
                hold(dve, s["dinv_made"], p)
                hold(dve, s["a0t_done"], p)
                for g in range(G):
                    last = dve.scalar_tensor_tensor(out=edges[:, g, :], in0=adj0[:, g, :], scalar=0.0, in1=ident[:, :],
                                                    op0=ALU.not_equal, op1=ALU.max, accum_out=nedges[:, g:g + 1])
                last.then_inc(s["edges_counted"], 1)
                dve.wait_ge(s["deg_summed"], p + 1)
                dve.tensor_scalar(degc[:, :], deg[:, :], DEG_EPS, None, ALU.max).then_inc(s["deg_clamped"], 1)
                dve.wait_ge(s["deg_clamped"], p + 1)
                hold(dve, s["adjn_made"], p)
                dve.reciprocal(rdeg[:, :], degc[:, :]).then_inc(s["deg_inverted"], 1)

            def norm_stats(layer, p, src, made, bn, aggr):
                dve.wait_ge(made, p + 1)
                for g in range(G):
                    last = dve.bn_stats(stats[:, layer, g, :], src[:, g, :])
                last.then_inc(bn, 1)
                stand_alone(dve)
                dve.wait_ge(bn, p + 1)
                for g in range(G):
                    last = dve.bn_aggr(mv[:, layer, g, :], stats[:, layer, g, :])
                last.then_inc(aggr, 1)

            def norm_apply(layer, p, dst, src, rstd_s, made):
                dve.wait_ge(rstd_s, p + 1)
                for g in range(G):
                    last = dve.tensor_scalar(dst[:, g, :], src[:, g, :], mv[:, layer, g, 0:1], rstd[:, layer, g:g + 1],
                                             ALU.subtract, ALU.mult)
                last.then_inc(made, 1)

            def ln0_stats(p):
                norm_stats(0, p, y0, s["y0_made"], s["bn0"], s["aggr0"])

            def ln0_apply(p):
                hold(dve, s["y1b_made"], p)
                hold(dve, s["y1_hi"], p)
                norm_apply(0, p, x1, y0, s["rstd0"], s["x1_made"])
                dve.wait_ge(s["dinv_made"], p + 1)
                dve.tensor_scalar(sdinv[:, :], dinv[:, :], 1.0 / WS, None, ALU.mult).then_inc(s["sdinv_made"], 1)

            def y1_low(p):
                dve.wait_ge(s["y1_hi"], p + 1)
                for g in range(G):
                    last = dve.scalar_tensor_tensor(out=y1[1][:, g, :], in0=x1[:, g, :], scalar=dinv[:, g:g + 1],
                                                    in1=y1[0][:, g, :], op0=ALU.mult, op1=ALU.subtract)
                last.then_inc(s["y1_lo"], 1)

            def before_tanh(p):
                dve.wait_ge(s["h1_done"], p + 1)
                dve.wait_ge(s["sdinv_made"], p + 1)
                for g in range(G):
                    last = dve.scalar_tensor_tensor(out=z1[:, g, :], in0=VB[:, g * F:(g + 1) * F], scalar=sdinv[:, g:g + 1],
                                                    in1=b1bc[:, :], op0=ALU.mult, op1=ALU.add)
                last.then_inc(s["z_made"], 1)

            def ln1_stats(p):
                norm_stats(1, p, y1b, s["y1b_made"], s["bn1"], s["aggr1"])

            def ln1_apply(p):
                hold(dve, s["xb_made"], p)
                norm_apply(1, p, x2, y1b, s["rstd1"], s["x2_made"])

            def masked_c(p):
                dve.wait_ge(s["c_rows"], p + 1)
                hold(dve, s["attn_made"], 4 * p)
                dve.tensor_tensor(c2[:, :, :], crow[:, :, :], maskbc[:, :, :], ALU.mult).then_inc(s["c_made"], 1)

            def query(p, h):
                dve.wait_ge(s["qk_done"], 4 * p + h + 1)
                if h == 0:
                    dve.wait_ge(s["mask_tiles"], p + 1)
                hold(dve, s["d_done"], 2 * p + h // 2 - 1)
                dve.scalar_tensor_tensor(out=qt[:, h], in0=half(QK, 0), scalar=-SCALE / WS, in1=maskbc[:, :, :],
                                         op0=ALU.mult, op1=ALU.mult).then_inc(s["q_made"], 1)

            def minus_max(p, u):
                dve.wait_ge(s["d_done"], 2 * p + u // 2 + 1)
                dve.tensor_reduce(negmax[:, u % 2, :], SC[u % 2][:, :].rearrange("p (a n) -> p a n", n=P), AX,
                                  ALU.min).then_inc(s["negmax_made"], 1)

            def normalise(p, u):
                dve.wait_ge(s["exps_made"], 4 * p + u + 1)
                dve.reciprocal(rrow[:, u % 2, :], rowsum[:, u % 2, :]).then_inc(s["rsum_made"], 1)
                dve.wait_ge(s["rsum_made"], 4 * p + u + 1)
                hold(dve, s["attn_made"], 4 * p + u - 1)
                dve.tensor_tensor(pn[:, u % 2], probs[:, u % 2],
                                  rrow[:, u % 2, :].unsqueeze(2).to_broadcast([P, 2 * G, P]), ALU.mult).then_inc(s["pn_made"], 1)

            def out_low(p, u):
                dve.wait_ge(s["ot_hi"], 4 * p + u + 1)
                dve.tensor_tensor(ot[1][:, u], half(TP, 0), ot[0][:, u], ALU.subtract).then_inc(s["ot_lo"], 1)

            def residual2(p):
                dve.wait_ge(s["wo_done"], p + 1)
                dve.wait_ge(s["xb_made"], p + 1)
                dve.scalar_tensor_tensor(out=y2[:, :, :], in0=v3(QK), scalar=1.0 / WS, in1=xb[:, :, :],
                                         op0=ALU.mult, op1=ALU.add).then_inc(s["y2_made"], 1)

            def ln2_stats(p):
                norm_stats(2, p, y2, s["y2_made"], s["bn2"], s["aggr2"])

            def ln2_apply(p):
                hold(dve, s["y3_made"], p)
                norm_apply(2, p, x3, y2, s["rstd2"], s["x3_made"])

            def exponent_shares(p):
                dve.wait_ge(s["x3_made"], p + 1)
                hold(dve, s["sj_hi"], p)
                for g in range(G):
                    last = dve.scalar_tensor_tensor(out=sjjunk[:, g, :], in0=x3[:, g, :], scalar=1.0, in1=wjrow[:, :],
                                                    op0=ALU.mult, op1=ALU.mult, accum_out=sj[:, g:g + 1])
                last.then_inc(s["sj_made"], 1)
                for g in range(G):
                    last = dve.scalar_tensor_tensor(out=sijunk[:, g, :], in0=x3[:, g, :], scalar=1.0, in1=wirow[:, :],
                                                    op0=ALU.mult, op1=ALU.mult, accum_out=sidot[:, g:g + 1])
                last.then_inc(s["sidot_made"], 1)
                dve.wait_ge(s["sidot_made"], p + 1)
                hold(dve, s["e_made"], p)
                dve.tensor_scalar(si[:, :], sidot[:, :], econst[:, :], None, ALU.add).then_inc(s["si_made"], 1)

            def share_low(p):
                dve.wait_ge(s["sj_hi"], p + 1)
                dve.tensor_tensor(sjrep[1][:, :, :], sj[:, :].unsqueeze(2).to_broadcast([P, G, P]), sjrep[0][:, :, :],
                                  ALU.subtract).then_inc(s["sj_lo"], 1)

            def leaky_relu(p):
                dve.wait_ge(s["e_made"], p + 1)
                hold(dve, s["expe_made"], p)
                dve.scalar_tensor_tensor(out=leaky[:, :, :], in0=ee[:, :, :], scalar=0.2, in1=ee[:, :, :],
                                         op0=ALU.mult, op1=ALU.max).then_inc(s["leaky_made"], 1)

            def transition(p):
                dve.wait_ge(s["expe_made"], p + 1)
                dve.wait_ge(s["adj3_loaded"], 16 * (p + 1))
                for g in range(G):
                    last = dve.scalar_tensor_tensor(out=mm[:, g, :], in0=expe[:, g, :], scalar=1.0, in1=adj3[:, g, :],
                                                    op0=ALU.mult, op1=ALU.mult, accum_out=ssum[:, g:g + 1])
                last.then_inc(s["m_made"], 1)
                dve.wait_ge(s["m_made"], p + 1)
                dve.tensor_scalar(ssume[:, :], ssum[:, :], SUM_EPS, None, ALU.add).then_inc(s["ssum_made"], 1)
                dve.wait_ge(s["ssum_made"], p + 1)
                dve.reciprocal(rs[:, :], ssume[:, :]).then_inc(s["rs_made"], 1)
                dve.wait_ge(s["rs_made"], p + 1)
                hold(dve, s["mt_done"], p)
                for g in range(G):
                    last = dve.tensor_scalar(tn[:, g, :], mm[:, g, :], rs[:, g:g + 1], WS, ALU.mult, ALU.mult)
                last.then_inc(s["tn_made"], 1)

            def transition_low(p):
                dve.wait_ge(s["tt_hi"], p + 1)
                dve.tensor_tensor(tt[1][:, :, :], half(O1, 0), tt[0][:, :, :], ALU.subtract).then_inc(s["tt_lo"], 1)

            def hop_low(p, src, dst, hi_made, made):
                dve.wait_ge(hi_made, p + 1)
                dve.scalar_tensor_tensor(out=dst[1][:, :, :], in0=v3(src), scalar=1.0 / WS, in1=dst[0][:, :, :],
                                         op0=ALU.mult, op1=ALU.subtract).then_inc(made, 1)

            def hops_plus_bias(p):
                dve.wait_ge(s["t0_done"], p + 1)
                hold(dve, s["relu3_made"], p)
                dve.scalar_tensor_tensor(out=hb[:, :, :], in0=v3(O3), scalar=1.0 / WS,
                                         in1=bksum2[:, :].unsqueeze(1).to_broadcast([P, G, F]),
                                         op0=ALU.mult, op1=ALU.add).then_inc(s["hb_made"], 1)

            def ln3_stats(p):
                norm_stats(3, p, y3, s["y3_made"], s["bn3"], s["aggr3"])

            def ln3_apply(p):
                hold(dve, s["out_stored"], 16 * p)
                norm_apply(3, p, xo, y3, s["rstd3"], s["xo_made"])

            def x0_low(p):
                rest(p, xt0[1], xt0[0], O1, s["xt0_hi"], s["xt0_lo"])

            def aggregate0_low(p):
                rest(p, agt[1], agt[0], O1, s["agt_hi"], s["agt_lo"])

            def aggregate1_low(p):
                rest(p, yt[1], yt[0], VB, s["yt_hi"], s["yt_lo"])

            def x2_low(p):
                rest(p, xt2[1], xt2[0], TP, s["xt2_hi"], s["xt2_lo"])

            def x3_low(p):
                rest(p, xt3[1], xt3[0], O1, s["xt3_hi"], s["xt3_lo"])

            def hop2_low(p):
                hop_low(p, O1, hw2, s["hw2_hi"], s["hw2_lo"])

            def hop1_low(p):
                hop_low(p, O2, u1, s["u1_hi"], s["u1_lo"])

            def step(t):
                go(minus_max, t, 2)
                go(out_low, t, 0)
                go(minus_max, t, 3)
                go(normalise, t, 2)
                go(transition_low, t - 1)
                go(aggregate1_low, t + 1)
                go(out_low, t, 1)
                go(degrees, t + 2)
                go(normalise, t, 3)
                go(before_tanh, t + 1)
                go(out_low, t, 2)
                go(hop1_low, t - 1)
                go(x0_low, t + 2)
                go(ln1_stats, t + 1)
                go(out_low, t, 3)
                go(aggregate0_low, t + 2)
                go(ln1_apply, t + 1)
                go(hops_plus_bias, t - 1)
                go(residual2, t)
                go(x2_low, t + 1)
                go(ln2_stats, t)
                go(masked_c, t + 1)
                go(query, t + 1, 0)
                go(ln3_stats, t - 1)
                go(ln2_apply, t)
                go(query, t + 1, 1)
                go(exponent_shares, t)
                go(ln0_stats, t + 2)
                go(share_low, t)
                go(x3_low, t)
                go(minus_max, t + 1, 0)
                go(ln3_apply, t - 1)
                go(leaky_relu, t)
                go(query, t + 1, 2)
                go(minus_max, t + 1, 1)
                go(normalise, t + 1, 0)
                go(ln0_apply, t + 2)
                go(query, t + 1, 3)
                go(normalise, t + 1, 1)
                go(y1_low, t + 2)
                go(transition, t)
                go(hop2_low, t)
            dve.wait_ge(s["ident_made"], 1)
            run(dve, step)

        @block.tensor
        def _(pe):
            def product(dst, lhs, rhs, k, first=False, last=False):
                for n, (i, j) in enumerate(((0, 0), (0, 1), (1, 0))):
                    mm_ = pe.matmul(dst, lhs(i, k), rhs(j, k), start=first and n == 0, stop=last and n == 2,
                                    skip_group_check=True)
                return mm_

            pe.wait_ge(s["ident_made"], 1)
            pe.wait_ge(s["raw0_loaded"], 16)
            for c in range(2 * FT):
                for o in range(FT):
                    dst = (DA, DB)[c // 2][:, (c % 2) * F + o * P:(c % 2) * F + (o + 1) * P]
                    last = pe.transpose(dst, raw0[:, o, c * P:(c + 1) * P], ident[:, :])
            last.then_inc(s["setup_psum"], 1)
            pe.wait_ge(s["rawv_loaded"], 16)
            for d in range(FT):
                for f in range(FT):
                    last = pe.transpose(O1[:, d * F + f * P:d * F + (f + 1) * P], rawv[:, f, d * P:(d + 1) * P], ident[:, :])
            last.then_inc(s["setup_psum"], 1)
            pe.wait_ge(s["setup_dve"], 5)
            pe.transpose(O3[:, 0:P], maskf[:, :], ident[:, :]).then_inc(s["setup_psum"], 1)
            pe.wait_ge(s["setup_moved"], 3)
            for d in range(FT):
                pe.matmul(O2[:, 0:F], arep[:, d, :], wvt[:, d, :], start=d == 0, stop=d == 1, skip_group_check=True)
            for d in range(FT):
                pe.matmul(O3[:, 128:384], arep[:, FT + d, :], wvt[:, d, :], start=d == 0, stop=d == 1, skip_group_check=True)
            for d in range(FT):
                last = pe.matmul(O3[:, 384:385], bvrep[:, d, :], asum[:, d:d + 1], start=False, stop=d == 1,
                                 skip_group_check=True)
            last.then_inc(s["setup_psum"], 1)
            pe.wait_ge(s["setup_lo"], 14)
            pe.wait_ge(s["setup_pool"], 4)

            def from_later(p, later, earlier):
                if isinstance(p, int) and p + AHEAD >= PAIRS:
                    hold(pe, earlier, p)
                else:
                    pe.wait_ge(later, p + AHEAD + 1)

            def from_earlier(p, earlier, before):
                if isinstance(p, int) and p <= AHEAD:
                    hold(pe, before, p)
                else:
                    pe.wait_ge(earlier, p - AHEAD)

            def transposes(p, src, dst, ready, done, n=1):
                pe.wait_ge(ready, n * (p + 1))
                for k in range(FT):
                    for g in range(G):
                        last = pe.transpose(dst[:, (k * G + g) * P:(k * G + g + 1) * P], src[:, g, k * P:(k + 1) * P], ident[:, :])
                last.then_inc(done, 1)

            def adjacency_transposed(p):
                pe.wait_ge(s["adjn_made"], p + 1)
                pe.wait_ge(s["edges_counted"], p + 1)
                from_earlier(p, s["u1_lo"], s["at_made"])
                for g in range(G):
                    pe.transpose(O2[:, g * P:(g + 1) * P], adjn[:, g, :], ident[:, :])
                for g in range(G):
                    last = pe.transpose(EDGES_T[:, g, :], edges[:, g, :], ident16[:, :])
                last.then_inc(s["a0t_done"], 1)

            def nodes_by_weights(p, dst, lhs, rhs, ks, first, wgt0=0):
                for g in range(G):
                    for k in ks:
                        last = product(dst[:, g * F:(g + 1) * F], lambda i, k: lhs[i][:, k, g, :],
                                       lambda j, k: rhs[j][:, wgt0 + k, :], k,
                                       first=first and g == 0 and k == ks[0], last=k == ks[-1])
                return last

            def aggregate0(p):
                pe.wait_ge(s["adjnt_made"], p + 1)
                pe.wait_ge(s["xt0_lo"], p + 1)
                for k in range(FT):
                    for g in range(G):
                        last = pe.matmul(O1[:, (k * G + g) * P:(k * G + g + 1) * P], x0[:, g, k * P:(k + 1) * P], adjnt[:, g, :],
                                         start=k == 0 and g == 0, stop=True, skip_group_check=True)
                last.then_inc(s["ag_done"], 1)

            def layer0_x(p):
                pe.wait_ge(s["xt0_lo"], p + 1)
                from_earlier(p, s["hb_made"], s["relu0_made"])
                nodes_by_weights(p, O3, xt0, w0t, range(FT), True)

            def layer0_agg(p):
                pe.wait_ge(s["agt_lo"], p + 1)
                nodes_by_weights(p, O3, agt, w0t, range(FT), False, wgt0=FT).then_inc(s["l0_done"], 1)

            def aggregate1(p):
                pe.wait_ge(s["y1_lo"], p + 1)
                pe.wait_ge(s["at_made"], p + 1)
                hold(pe, s["v_made"], 2 * p)
                for k in range(FT):
                    for g in range(G):
                        for n in range(2):
                            last = pe.matmul(VB[:, (k * G + g) * P:(k * G + g + 1) * P], y1[n][:, g, k * P:(k + 1) * P],
                                             at[:, g, :], start=k == 0 and g == 0 and n == 0, stop=n == 1,
                                             skip_group_check=True)
                last.then_inc(s["ya_done"], 1)

            def layer1(p):
                pe.wait_ge(s["yt_lo"], p + 1)
                nodes_by_weights(p, VB, yt, w1p, range(FT), True).then_inc(s["h1_done"], 1)

            def project_qk(p, h):
                if h == 0:
                    pe.wait_ge(s["xt2_lo"], p + 1)
                    hold(pe, s["y2_made"], p)
                else:
                    pe.wait_ge(s["k_made"], 4 * p + h)
                for part, w in enumerate((wq, wkk)):
                    for k in range(FT):
                        last = product(QK[:, part * 256:(part + 1) * 256], lambda i, k: w[i][:, k, h, :],
                                       lambda j, k: xt2[j][:, k].rearrange("p g n -> p (g n)"), k,
                                       first=part == 0 and k == 0, last=k == FT - 1)
                last.then_inc(s["qk_done"], 1)

            def project_v(p, g):
                if g == 0:
                    pe.wait_ge(s["xt2_lo"], p + 1)
                    pe.wait_ge(s["z_made"], p + 1)
                else:
                    pe.wait_ge(s["v_made"], 2 * p + 1)
                for k in range(FT):
                    last = product(VB[:, :], lambda i, k: xt2[i][:, k, g, :], lambda j, k: wvv[j][:, k, :], k,
                                   first=k == 0, last=k == FT - 1)
                last.then_inc(s["v_done"], 1)

            def scores(p, j):
                if j == 0:
                    pe.wait_ge(s["mask_rows"], p + 1)
                pe.wait_ge(s["k_made"], 4 * p + 2 * j + 2)
                hold(pe, s["exps_made"], 4 * p + 2 * j)
                for g in range(G):
                    for e in range(2):
                        pe.matmul(SC[e][:, g * 256:(g + 1) * 256], maskrow[e * DH:e * DH + 1, g, :],
                                  bigrow[e * DH:e * DH + 1, g:g + 1, :].to_broadcast([1, 2, P]), start=g == 0, stop=False,
                                  skip_group_check=True)
                for g in range(G):
                    for l in range(2):
                        for e in range(2):
                            rows = slice(e * DH, (e + 1) * DH)
                            last = pe.matmul(SC[e][:, (2 * g + l) * P:(2 * g + l + 1) * P], qt[rows, 2 * j + l, g, :],
                                             kt[rows, 2 * j + l, g, :], start=False, stop=True, skip_group_check=True)
                last.then_inc(s["d_done"], 1)

            def attention_transposed(p, u):
                pe.wait_ge(s["attn_made"], 4 * p + u + 1)
                if u > 0:
                    pe.wait_ge(s["ot_lo"], 4 * p + u)
                for g in range(G):
                    for l in range(2):
                        last = pe.transpose(TP[:, (2 * g + l) * P:(2 * g + l + 1) * P], attn[:, u % 2, g, l, :], ident[:, :])
                last.then_inc(s["tr_done"], 1)

            def apply_attention(p, u):
                pe.wait_ge(s["pt_made"], 4 * p + u + 1)
                if u == 0:
                    pe.wait_ge(s["v_made"], 2 * p + 2)
                for g in range(G):
                    for l in range(2):
                        head = 4 * (u // 2) + 2 * l + u % 2
                        last = pe.matmul(TP[l * DH:(l + 1) * DH, g * P:(g + 1) * P], vv[:, g, head * DH:(head + 1) * DH],
                                         pt[:, g, l, :], start=True, stop=True, skip_group_check=True)
                last.then_inc(s["pv_done"], 1)

            def project_out(p):
                pe.wait_ge(s["ot_lo"], 4 * p + 4)
                pe.wait_ge(s["k_made"], 4 * p + 4)
                for g in range(G):
                    for k in range(HP):
                        last = product(QK[:, g * F:(g + 1) * F], lambda i, k: ot[i][:, k, g, :], lambda j, k: wo[j][:, k, :], k,
                                       first=g == 0 and k == 0, last=k == HP - 1)
                last.then_inc(s["wo_done"], 1)

            def exponents(p):
                pe.wait_ge(s["sj_lo"], p + 1)
                from_later(p, s["at_made"], s["u1_lo"])
                for g in range(G):
                    for n in range(2):
                        last = pe.matmul(O2[:, g * P:(g + 1) * P], sjrep[n][:, g, :], ident16[:, :],
                                         start=g == 0 and n == 0, stop=n == 1, skip_group_check=True)
                last.then_inc(s["e3_done"], 1)

            def hop(dst, n):
                for g in range(G):
                    for k in range(FT):
                        last = product(dst[:, g * F:(g + 1) * F], lambda i, k: xt3[i][:, k, g, :], lambda j, k: wl[j][:, k, n, :], k,
                                       first=g == 0 and k == 0, last=k == FT - 1)
                return last

            def hop1_product(p):
                pe.wait_ge(s["xt3_lo"], p + 1)
                pe.wait_ge(s["e_made"], p + 1)
                hop(O2, 1)

            def hop0_product(p):
                from_later(p, s["relu0_made"], s["hb_made"])
                hop(O3, 0)

            def transition_transposed(p):
                pe.wait_ge(s["tn_made"], p + 1)
                pe.wait_ge(s["hw2_lo"], p + 1)
                for g in range(G):
                    last = pe.transpose(O1[:, g * P:(g + 1) * P], tn[:, g, :], ident[:, :])
                last.then_inc(s["mt_done"], 1)

            def diffuse(p, dst, src, ready, done):
                pe.wait_ge(ready, p + 1)
                for g in range(G):
                    last = product(dst[:, g * F:(g + 1) * F], lambda i, k: tt[i][:, g, :], lambda j, k: src[j][:, g, :], 0,
                                   last=True)
                last.then_inc(done, 1)

            def x0_transposed(p):
                from_earlier(p, s["tt_lo"], s["agt_lo"])
                transposes(p, x0, O1, s["x0_loaded"], s["x0t_done"], 16)

            def x2_transposed(p):
                hold(pe, s["ot_lo"], 4 * p)
                transposes(p, x2, TP, s["x2_made"], s["xt2_done"])

            def x3_transposed(p):
                from_later(p, s["agt_lo"], s["tt_lo"])
                transposes(p, x3, O1, s["x3_made"], s["xt3_done"])

            def hop2_product(p):
                pe.wait_ge(s["xt3_lo"], p + 1)
                hop(O1, 2).then_inc(s["w2_done"], 1)

            def diffuse1(p):
                pe.wait_ge(s["tt_lo"], p + 1)
                diffuse(p, O2, hw2, s["hw2_lo"], s["t1_done"])

            def diffuse0(p):
                diffuse(p, O3, u1, s["u1_lo"], s["t0_done"])

            def step(t):
                go(apply_attention, t, 0)
                go(hop1_product, t - 1)
                go(attention_transposed, t, 1)
                go(transition_transposed, t - 1)
                go(aggregate1, t + 1)
                go(apply_attention, t, 1)
                go(x0_transposed, t + 2)
                go(diffuse1, t - 1)
                go(attention_transposed, t, 2)
                go(layer1, t + 1)
                go(apply_attention, t, 2)
                go(hop0_product, t - 1)
                go(attention_transposed, t, 3)
                go(adjacency_transposed, t + 2)
                go(diffuse0, t - 1)
                go(apply_attention, t, 3)
                go(aggregate0, t + 2)
                go(project_out, t)
                go(x2_transposed, t + 1)
                go(layer0_x, t + 2)
                go(project_qk, t + 1, 0)
                go(layer0_agg, t + 2)
                go(project_qk, t + 1, 1)
                go(project_v, t + 1, 0)
                go(x3_transposed, t)
                go(scores, t + 1, 0)
                go(exponents, t)
                go(project_qk, t + 1, 2)
                go(hop2_product, t)
                go(project_qk, t + 1, 3)
                go(project_v, t + 1, 1)
                go(attention_transposed, t + 1, 0)
                go(scores, t + 1, 1)
            run(pe, step)


_INS = ["x", "adj", "nodemask", "L0_gnn_W", "L1_gnn_W", "L1_gnn_b", "L2_gnn_W_qkv", "L2_gnn_W_out", "L2_gnn_b_out",
        "L3_gnn_Wv", "L3_gnn_bv", "L3_gnn_aw", "L3_gnn_ab", "L3_gnn_Wk", "L3_gnn_bk"]


def kernel(**inputs):
    import numpy as _np
    import concourse.bacc as _bacc
    from concourse import mybir as _mybir
    from concourse.bass_utils import run_bass_kernel_spmd as _run

    nc = _bacc.Bacc("TRN2", target_bir_lowering=False, num_devices=1)
    arrays, args = {}, []
    for name in _INS:
        a = _np.ascontiguousarray(inputs[name])
        if a.dtype == _np.bool_:
            a = a.view(_np.uint8)
        arrays[f"in_{name}"] = a
        args.append(nc.dram_tensor(f"in_{name}", a.shape, _mybir.dt.from_np(a.dtype), kind="ExternalInput").ap())
    out = nc.dram_tensor("out_0", inputs["x"].shape, _mybir.dt.float32, kind="ExternalOutput").ap()
    build(nc, *args, out)
    r = _run(nc, [arrays], core_ids=[0])
    return r.results[0]["out_0"]
```
